# Optimizing a Trainium2 kernel written in Bass

```python
import numpy as np
import jax
import jax.numpy as jnp

def _softmax(x, axis=-1):
    return jax.nn.softmax(x, axis=axis)

def _gelu(x):
    return jax.nn.gelu(x, approximate=True)

def _silu(x):
    return jax.nn.silu(x)

def _sigmoid(x):
    return jax.nn.sigmoid(x)

def _layernorm(x, axis=-1, eps=1e-05):
    m = jnp.mean(x, axis=axis, keepdims=True)
    v = jnp.var(x, axis=axis, keepdims=True)
    return (x - m) / jnp.sqrt(v + eps)

def _scatter_add(tgt, idx, src, axis=0):
    return tgt.at[idx].add(src)

def _segment_sum(src, seg, n):
    return jax.ops.segment_sum(src, seg, n)
kernel_name = 'mk_dlrm_tower_d1_rec_r8_71768f'

def setup_inputs(seed: int=0):
    np.random.seed(seed)
    _w = jnp.asarray

    def _rec_inputs():
        import jax
        import jax.numpy as jnp
        _tk = jax.random.key(seed)
        dense_ctx = jax.random.normal(jax.random.fold_in(_tk, 190), (512, 16), jnp.float32)
        ids = jnp.stack([jax.random.randint(jax.random.fold_in(_tk, 200 + f), (512,), 0, v, jnp.int32) for f, v in enumerate([1000, 1000, 12500, 125000, 1000, 125000, 1000, 1000, 125000, 1250, 12500, 12500, 12500, 1000, 1250, 1000, 1250, 1250, 1250, 1250, 12500, 1000, 1000, 1000, 1000, 1000, 12500, 1250, 1000, 1250, 12500, 1250])], axis=1)
        tbl_0 = 0.05 * jax.random.normal(jax.random.fold_in(_tk, 500 + 0), (1000, 64), jnp.float32)
        tbl_1 = 0.05 * jax.random.normal(jax.random.fold_in(_tk, 500 + 1), (1000, 64), jnp.float32)
        tbl_2 = 0.05 * jax.random.normal(jax.random.fold_in(_tk, 500 + 2), (12500, 64), jnp.float32)
        tbl_3 = 0.05 * jax.random.normal(jax.random.fold_in(_tk, 500 + 3), (125000, 64), jnp.float32)
        tbl_4 = 0.05 * jax.random.normal(jax.random.fold_in(_tk, 500 + 4), (1000, 64), jnp.float32)
        tbl_5 = 0.05 * jax.random.normal(jax.random.fold_in(_tk, 500 + 5), (125000, 64), jnp.float32)
        tbl_6 = 0.05 * jax.random.normal(jax.random.fold_in(_tk, 500 + 6), (1000, 64), jnp.float32)
        tbl_7 = 0.05 * jax.random.normal(jax.random.fold_in(_tk, 500 + 7), (1000, 64), jnp.float32)
        tbl_8 = 0.05 * jax.random.normal(jax.random.fold_in(_tk, 500 + 8), (125000, 64), jnp.float32)
        tbl_9 = 0.05 * jax.random.normal(jax.random.fold_in(_tk, 500 + 9), (1250, 64), jnp.float32)
        tbl_10 = 0.05 * jax.random.normal(jax.random.fold_in(_tk, 500 + 10), (12500, 64), jnp.float32)
        tbl_11 = 0.05 * jax.random.normal(jax.random.fold_in(_tk, 500 + 11), (12500, 64), jnp.float32)
        tbl_12 = 0.05 * jax.random.normal(jax.random.fold_in(_tk, 500 + 12), (12500, 64), jnp.float32)
        tbl_13 = 0.05 * jax.random.normal(jax.random.fold_in(_tk, 500 + 13), (1000, 64), jnp.float32)
        tbl_14 = 0.05 * jax.random.normal(jax.random.fold_in(_tk, 500 + 14), (1250, 64), jnp.float32)
        tbl_15 = 0.05 * jax.random.normal(jax.random.fold_in(_tk, 500 + 15), (1000, 64), jnp.float32)
        tbl_16 = 0.05 * jax.random.normal(jax.random.fold_in(_tk, 500 + 16), (1250, 64), jnp.float32)
        tbl_17 = 0.05 * jax.random.normal(jax.random.fold_in(_tk, 500 + 17), (1250, 64), jnp.float32)
        tbl_18 = 0.05 * jax.random.normal(jax.random.fold_in(_tk, 500 + 18), (1250, 64), jnp.float32)
        tbl_19 = 0.05 * jax.random.normal(jax.random.fold_in(_tk, 500 + 19), (1250, 64), jnp.float32)
        tbl_20 = 0.05 * jax.random.normal(jax.random.fold_in(_tk, 500 + 20), (12500, 64), jnp.float32)
        tbl_21 = 0.05 * jax.random.normal(jax.random.fold_in(_tk, 500 + 21), (1000, 64), jnp.float32)
        tbl_22 = 0.05 * jax.random.normal(jax.random.fold_in(_tk, 500 + 22), (1000, 64), jnp.float32)
        tbl_23 = 0.05 * jax.random.normal(jax.random.fold_in(_tk, 500 + 23), (1000, 64), jnp.float32)
        tbl_24 = 0.05 * jax.random.normal(jax.random.fold_in(_tk, 500 + 24), (1000, 64), jnp.float32)
        tbl_25 = 0.05 * jax.random.normal(jax.random.fold_in(_tk, 500 + 25), (1000, 64), jnp.float32)
        tbl_26 = 0.05 * jax.random.normal(jax.random.fold_in(_tk, 500 + 26), (12500, 64), jnp.float32)
        tbl_27 = 0.05 * jax.random.normal(jax.random.fold_in(_tk, 500 + 27), (1250, 64), jnp.float32)
        tbl_28 = 0.05 * jax.random.normal(jax.random.fold_in(_tk, 500 + 28), (1000, 64), jnp.float32)
        tbl_29 = 0.05 * jax.random.normal(jax.random.fold_in(_tk, 500 + 29), (1250, 64), jnp.float32)
        tbl_30 = 0.05 * jax.random.normal(jax.random.fold_in(_tk, 500 + 30), (12500, 64), jnp.float32)
        tbl_31 = 0.05 * jax.random.normal(jax.random.fold_in(_tk, 500 + 31), (1250, 64), jnp.float32)
        _rk = jax.random.fold_in(_tk, 7)
        W_top1 = 0.0441942 * jax.random.normal(jax.random.fold_in(_tk, 801), (512, 512), jnp.float32)
        W_top2 = 0.0441942 * jax.random.normal(jax.random.fold_in(_tk, 802), (512, 256), jnp.float32)
        W_top3 = 0.0625 * jax.random.normal(jax.random.fold_in(_tk, 803), (256, 1), jnp.float32)
        b_top1 = jnp.zeros((512,), jnp.float32)
        b_top2 = jnp.zeros((256,), jnp.float32)
        return (dense_ctx, ids, tbl_0, tbl_1, tbl_2, tbl_3, tbl_4, tbl_5, tbl_6, tbl_7, tbl_8, tbl_9, tbl_10, tbl_11, tbl_12, tbl_13, tbl_14, tbl_15, tbl_16, tbl_17, tbl_18, tbl_19, tbl_20, tbl_21, tbl_22, tbl_23, tbl_24, tbl_25, tbl_26, tbl_27, tbl_28, tbl_29, tbl_30, tbl_31, W_top1, b_top1, W_top2, b_top2, W_top3)
    dense_ctx, ids, tbl_0, tbl_1, tbl_2, tbl_3, tbl_4, tbl_5, tbl_6, tbl_7, tbl_8, tbl_9, tbl_10, tbl_11, tbl_12, tbl_13, tbl_14, tbl_15, tbl_16, tbl_17, tbl_18, tbl_19, tbl_20, tbl_21, tbl_22, tbl_23, tbl_24, tbl_25, tbl_26, tbl_27, tbl_28, tbl_29, tbl_30, tbl_31, W_top1, b_top1, W_top2, b_top2, W_top3 = _rec_inputs()

    def _L0_rec_setup():
        import jax, jax.numpy as jnp
        import numpy as np
        FIELDS = 32
        EMBED = 64
        BATCH = 1024
        PAIR = FIELDS * (FIELDS - 1) // 2

        def _pair_ids(fields):
            pairs = np.array([(i, j) for i in range(fields - 1) for j in range(i + 1, fields)], dtype=np.int32)
            return (jnp.asarray(pairs[:, 0]), jnp.asarray(pairs[:, 1]))
        key = jax.random.key(seed)
        k1, k2 = jax.random.split(key)
        inputs = jax.random.normal(k1, (BATCH, FIELDS, EMBED), dtype=jnp.float32)
        w = 0.05 * jax.random.normal(k2, (PAIR, EMBED, EMBED), dtype=jnp.float32)
        return {'inputs': inputs, 'w': w}
    _L0_rec_all = _L0_rec_setup()
    _L0_rec_in = {k: v for k, v in _L0_rec_all.items() if k in ('w',)}
    del _L0_rec_all
    return {'dense_ctx': dense_ctx, 'ids': ids, 'tbl_0': tbl_0, 'tbl_1': tbl_1, 'tbl_2': tbl_2, 'tbl_3': tbl_3, 'tbl_4': tbl_4, 'tbl_5': tbl_5, 'tbl_6': tbl_6, 'tbl_7': tbl_7, 'tbl_8': tbl_8, 'tbl_9': tbl_9, 'tbl_10': tbl_10, 'tbl_11': tbl_11, 'tbl_12': tbl_12, 'tbl_13': tbl_13, 'tbl_14': tbl_14, 'tbl_15': tbl_15, 'tbl_16': tbl_16, 'tbl_17': tbl_17, 'tbl_18': tbl_18, 'tbl_19': tbl_19, 'tbl_20': tbl_20, 'tbl_21': tbl_21, 'tbl_22': tbl_22, 'tbl_23': tbl_23, 'tbl_24': tbl_24, 'tbl_25': tbl_25, 'tbl_26': tbl_26, 'tbl_27': tbl_27, 'tbl_28': tbl_28, 'tbl_29': tbl_29, 'tbl_30': tbl_30, 'tbl_31': tbl_31, 'W_top1': W_top1, 'b_top1': b_top1, 'W_top2': W_top2, 'b_top2': b_top2, 'W_top3': W_top3, 'L0_rec_w': _L0_rec_in['w']}

def reference(dense_ctx, ids, tbl_0, tbl_1, tbl_2, tbl_3, tbl_4, tbl_5, tbl_6, tbl_7, tbl_8, tbl_9, tbl_10, tbl_11, tbl_12, tbl_13, tbl_14, tbl_15, tbl_16, tbl_17, tbl_18, tbl_19, tbl_20, tbl_21, tbl_22, tbl_23, tbl_24, tbl_25, tbl_26, tbl_27, tbl_28, tbl_29, tbl_30, tbl_31, W_top1, b_top1, W_top2, b_top2, W_top3, L0_rec_w):
    import jax
    import jax.numpy as jnp

    def _L0_rec_ref(inputs, w):
        import jax, jax.numpy as jnp
        import numpy as np
        FIELDS = 32
        EMBED = 64
        BATCH = 1024
        PAIR = FIELDS * (FIELDS - 1) // 2

        def _pair_ids(fields):
            pairs = np.array([(i, j) for i in range(fields - 1) for j in range(i + 1, fields)], dtype=np.int32)
            return (jnp.asarray(pairs[:, 0]), jnp.asarray(pairs[:, 1]))
        ids_x, ids_y = _pair_ids(FIELDS)
        p = inputs[:, ids_x, :]
        q = inputs[:, ids_y, :]
        pw = jnp.einsum('bpi,pij->bpj', p, w)
        out = jnp.einsum('bpj,bpj->bp', pw, q)
        return out
    e = jnp.stack([tbl_0[ids[:, 0]], tbl_1[ids[:, 1]], tbl_2[ids[:, 2]], tbl_3[ids[:, 3]], tbl_4[ids[:, 4]], tbl_5[ids[:, 5]], tbl_6[ids[:, 6]], tbl_7[ids[:, 7]], tbl_8[ids[:, 8]], tbl_9[ids[:, 9]], tbl_10[ids[:, 10]], tbl_11[ids[:, 11]], tbl_12[ids[:, 12]], tbl_13[ids[:, 13]], tbl_14[ids[:, 14]], tbl_15[ids[:, 15]], tbl_16[ids[:, 16]], tbl_17[ids[:, 17]], tbl_18[ids[:, 18]], tbl_19[ids[:, 19]], tbl_20[ids[:, 20]], tbl_21[ids[:, 21]], tbl_22[ids[:, 22]], tbl_23[ids[:, 23]], tbl_24[ids[:, 24]], tbl_25[ids[:, 25]], tbl_26[ids[:, 26]], tbl_27[ids[:, 27]], tbl_28[ids[:, 28]], tbl_29[ids[:, 29]], tbl_30[ids[:, 30]], tbl_31[ids[:, 31]]], axis=1)
    z = _L0_rec_ref(e, L0_rec_w)
    z = z.reshape(z.shape[0], -1)
    h = jnp.concatenate([z, dense_ctx], axis=1)
    h = jnp.maximum(h @ W_top1 + b_top1, 0.0)
    h = jnp.maximum(h @ W_top2 + b_top2, 0.0)
    y = h @ W_top3
    return y

_drawn_inputs = setup_inputs


def setup_inputs(seed=0):
    import zlib

    import numpy as np

    out = dict(_drawn_inputs(seed))
    spreads = {'b_top1': (0.0, 0.1), 'b_top2': (0.0, 0.1)}
    factors = {'tbl_0': 6.744,
     'tbl_1': 6.231,
     'tbl_2': 5.87,
     'tbl_3': 6.086,
     'tbl_4': 5.059,
     'tbl_5': 6.46,
     'tbl_6': 5.886,
     'tbl_7': 4.971,
     'tbl_8': 5.953,
     'tbl_9': 5.94,
     'tbl_10': 5.547,
     'tbl_11': 5.517,
     'tbl_12': 5.03,
     'tbl_13': 5.198,
     'tbl_14': 5.807,
     'tbl_15': 5.828,
     'tbl_16': 5.406,
     'tbl_17': 6.161,
     'tbl_18': 5.416,
     'tbl_19': 5.795,
     'tbl_20': 5.547,
     'tbl_21': 5.845,
     'tbl_22': 5.96,
     'tbl_23': 5.466,
     'tbl_24': 6.009,
     'tbl_25': 5.668,
     'tbl_26': 5.836,
     'tbl_27': 5.586,
     'tbl_28': 5.963,
     'tbl_29': 6.116,
     'tbl_30': 5.93,
     'tbl_31': 6.608}
    for name, (base, spread) in spreads.items():
        noise = np.random.default_rng([zlib.crc32(name.encode()), seed]).standard_normal(out[name].shape)
        drawn = base * np.exp(spread * noise) if base else spread * noise
        out[name] = jnp.asarray(drawn.astype(out[name].dtype))
    for name, factor in factors.items():
        out[name] = (out[name] * factor).astype(out[name].dtype)
    return out
```

```python
from contextlib import ExitStack

import concourse.bass as bass
import numpy as np
from concourse import mybir

FIELDS = 32
EMBED = 64
BATCH = 512
DENSE = 16
HIDDEN1 = 512
HIDDEN2 = 256
P = 128
BLOCKS = BATCH // P
COUPLES = FIELDS // 2
PAIRS = FIELDS * (FIELDS - 1) // 2

CHUNK = 8
CHUNK_COLS = CHUNK * P
RAW_RING = 3
SPLIT_RING = 5
PRODUCT_RING = 4
GATHER_RING = 4
PARTNER_RING = 3
WEIGHT_LEAD = 8


def pair_index(i, j):
    return i * (FIELDS - 1) - i * (i - 1) // 2 + (j - i - 1)


def build_plan():
    groups, slots, first_group = [], [], {}
    for m in range(COUPLES):
        first_group[m] = len(groups)
        for i in range(0, 2 * m, 2):
            tiles = []
            for field in (i, i + 1):
                halves = (pair_index(field, 2 * m), pair_index(field, 2 * m + 1))
                tiles.append((halves, [(len(slots), field)]))
                slots.append(halves)
            groups.append((m, tiles))
        if m % 4 == 3:
            tiles = []
            for q in (m // 2 - 1, m // 2):
                halves = (pair_index(4 * q, 4 * q + 1), pair_index(4 * q + 2, 4 * q + 3))
                tiles.append((halves, [(len(slots), 4 * q), (len(slots) + 1, 4 * q + 2)]))
                slots += [(halves[0], PAIRS), (PAIRS, halves[1])]
            groups.append((None, tiles))
    return groups, slots, first_group


GROUPS, SLOTS, FIRST_GROUP = build_plan()
N_GROUPS = len(GROUPS)
N_CHUNKS = len(SLOTS) // CHUNK
N_TILES = 2 * N_GROUPS
COL_TILES = 4
Z_TILE_STEPS = 16
BATCHES = N_TILES // COL_TILES
Z_TILES = -(-BATCHES // Z_TILE_STEPS)
LAST_STEPS = BATCHES - (Z_TILES - 1) * Z_TILE_STEPS
FREE_ROWS = 32 - 2 * LAST_STEPS


def z_place(tile, half):
    batch, quadrant = divmod(tile, COL_TILES)
    return batch // Z_TILE_STEPS, 32 * quadrant + 2 * (batch % Z_TILE_STEPS) + half


def slots_of(group):
    return [slot for _, passes in GROUPS[group][1] for slot, _ in passes]


CHUNK_FIRST = [min(g for g in range(N_GROUPS) if c in [s // CHUNK for s in slots_of(g)]) for c in range(N_CHUNKS)]
CHUNK_LAST = [max(g for g in range(N_GROUPS) if c in [s // CHUNK for s in slots_of(g)]) for c in range(N_CHUNKS)]


def couple_step(m):
    if m <= 1:
        return 0
    return FIRST_GROUP[m] - (0 if m <= 6 else 2)


COUPLE_AT = {g: [m for m in range(COUPLES) if couple_step(m) == g] for g in range(N_GROUPS)}
CHUNK_AT = {g: [c for c in range(N_CHUNKS) if max(0, CHUNK_FIRST[c] - WEIGHT_LEAD) == g] for g in range(N_GROUPS)}
LAST_OF_COUPLE = {m: max(g for g in range(N_GROUPS) if GROUPS[g][0] == m) for m in range(1, COUPLES)}
DIAGONAL = [g for g in range(N_GROUPS) if GROUPS[g][0] is None]


def build_tower(nc, ids, tables, weights, w1, b1, w2, b2, w3, dense, out):
    fp32 = mybir.dt.float32
    fp32r = mybir.dt.float32r
    int32 = mybir.dt.int32
    ALU = mybir.AluOpType
    ACT = mybir.ActivationFunctionType

    ctx = ExitStack()
    with ctx:

        def sb(name, shape, dt=fp32):
            return ctx.enter_context(nc.sbuf_tensor(name, shape, dt))

        def pb(name, shape):
            return ctx.enter_context(nc.psum_tensor(name, shape, fp32))

        def sem(name):
            return ctx.enter_context(nc.semaphore(name))

        ids_sb = sb("ids_sb", [P, BLOCKS, FIELDS], int32)
        rows = sb("rows", [P, GATHER_RING, BLOCKS, 2 * EMBED])
        parts = sb("parts", [P, 2, BLOCKS, 2, 2, EMBED], fp32r)
        moving = sb("moving", [P, FIELDS, BATCH], fp32r)
        partner = sb("partner", [P, PARTNER_RING, BATCH])
        odd = sb("odd", [P, 2, BATCH])
        w_raw = sb("w_raw", [P, RAW_RING, CHUNK_COLS])
        w_hi = sb("w_hi", [P, SPLIT_RING, CHUNK, P], fp32r)
        w_lo = sb("w_lo", [P, SPLIT_RING, CHUNK, P], fp32r)
        product = sb("product", [P, PRODUCT_RING, 2, BATCH])
        selector = sb("selector", [P, Z_TILE_STEPS, 32])
        identity = sb("identity", [P, P])
        z = sb("z", [P, Z_TILES, BATCH])
        w1_sb = sb("w1_sb", [P, Z_TILES, HIDDEN1])
        w2_sb = sb("w2_sb", [P, HIDDEN1 // P, HIDDEN2])
        w3_sb = sb("w3_sb", [P, HIDDEN2 // P])
        b1_sb = sb("b1_sb", [P, HIDDEN1 // P])
        b2_sb = sb("b2_sb", [P, HIDDEN2 // P])
        h1 = sb("h1", [P, HIDDEN1 // P, BATCH])
        h2 = sb("h2", [P, HIDDEN2 // P, BATCH])
        y = sb("y", [1, BATCH])

        projected = pb("projected", [P, 2, 2, BATCH])
        turned = pb("turned", [P, 2, BATCH])
        z_sum = pb("z_sum", [P, 2, BATCH])

        ids_loaded = sem("ids_loaded")
        mlp_loaded = sem("mlp_loaded")
        rows_gathered = [sem(f"rows_gathered_{k}") for k in range(GATHER_RING)]
        w_loaded = [sem(f"w_loaded_{k}") for k in range(RAW_RING)]
        zeroed = sem("zeroed")
        constants_made = sem("constants_made")
        selector_zeroed = sem("selector_zeroed")
        selector_made = sem("selector_made")
        w_hi_made = sem("w_hi_made")
        w_lo_made = sem("w_lo_made")
        e_hi_made = sem("e_hi_made")
        e_lo_made = sem("e_lo_made")
        turn_done = sem("turn_done")
        turn_copied = sem("turn_copied")
        odd_made = sem("odd_made")
        project_done = sem("project_done")
        multiply_done = sem("multiply_done")
        reduce_done = sem("reduce_done")
        z_copied = sem("z_copied")
        h1_summed = sem("h1_summed")
        h1_made = sem("h1_made")
        h2_summed = sem("h2_summed")
        h2_made = sem("h2_made")
        y_summed = sem("y_summed")
        y_made = sem("y_made")
        y_stored = sem("y_stored")

        def rows_ready(m):
            return rows_gathered[m % GATHER_RING], 16 * 2 * BLOCKS * (m // GATHER_RING + 1)

        def raw_ready(c):
            return w_loaded[c % RAW_RING], 32 * (c // RAW_RING + 1)

        block = ctx.enter_context(nc.Block())

        @block.sync
        def _(sp):
            sp.dma_start(ids_sb[:], ids).then_inc(ids_loaded, 16)
            for c in range(N_CHUNKS):
                if c >= RAW_RING:
                    sp.wait_ge(w_hi_made, c - RAW_RING + 1)
                    sp.wait_ge(w_lo_made, c - RAW_RING + 1)
                for half in (0, 1):
                    sp.dma_start(
                        w_raw[half * EMBED : (half + 1) * EMBED, c % RAW_RING, :],
                        weights[:, c * CHUNK_COLS : (c + 1) * CHUNK_COLS],
                    ).then_inc(w_loaded[c % RAW_RING], 16)
                if c == 6:
                    sp.dma_start(w1_sb[:], w1).then_inc(mlp_loaded, 16)
                    sp.dma_start(w2_sb[:], w2).then_inc(mlp_loaded, 16)
                    sp.dma_start(w3_sb[:], w3).then_inc(mlp_loaded, 16)
                    sp.dma_start(b1_sb[:], b1).then_inc(mlp_loaded, 16)
                    sp.dma_start(b2_sb[:], b2).then_inc(mlp_loaded, 16)
                    for quadrant in range(COL_TILES):
                        row = 32 * quadrant + 2 * LAST_STEPS
                        sp.dma_start(
                            z[row : row + FREE_ROWS, Z_TILES - 1, :],
                            dense[quadrant * FREE_ROWS : (quadrant + 1) * FREE_ROWS, :],
                        ).then_inc(mlp_loaded, 16)
            sp.wait_ge(y_made, 1)
            sp.dma_start(out, y[:]).then_inc(y_stored, 16)
            sp.wait_ge(y_stored, 16)

        @block.gpsimd
        def _(pool):
            pool.memset(identity[:], 0.0).then_inc(zeroed, 1)
            pool.wait_ge(zeroed, 1)
            nc.gpsimd.affine_select(
                out=identity[:], in_=identity[:], compare_op=ALU.not_equal, fill=1.0,
                base=0, pattern=[[-1, P]], channel_multiplier=1,
            ).then_inc(constants_made, 1)
            pool.wait_ge(ids_loaded, 16)
            for m in range(COUPLES):
                if m >= GATHER_RING:
                    pool.wait_ge(e_hi_made, m - GATHER_RING + 1)
                    pool.wait_ge(e_lo_made, m - GATHER_RING + 1)
                    pool.wait_ge(turn_done, 3 * (m - GATHER_RING) + 1)
                for field in (2 * m, 2 * m + 1):
                    for b in range(BLOCKS):
                        col = (field % 2) * EMBED
                        nc.gpsimd.indirect_dma_start(
                            rows[:, m % GATHER_RING, b, col : col + EMBED], None,
                            tables[field],
                            bass.IndirectOffsetOnAxis(ap=ids_sb[:, b, field : field + 1], axis=0),
                        ).then_inc(rows_gathered[m % GATHER_RING], 16)

        @block.scalar
        def _(act):
            def split_weights_hi(c):
                act.wait_ge(*raw_ready(c))
                if c >= SPLIT_RING:
                    act.wait_ge(project_done, CHUNK_LAST[c - SPLIT_RING] + 1)
                nc.scalar.activation(
                    w_hi[:, c % SPLIT_RING, :, :].rearrange("p s c -> p (s c)"), w_raw[:, c % RAW_RING, :], ACT.Copy
                ).then_inc(w_hi_made, 1)

            def split_rows_hi(m):
                act.wait_ge(*rows_ready(m))
                if m >= 2:
                    act.wait_ge(turn_done, 3 * (m - 2) + 3)
                nc.scalar.activation(
                    parts[:, m % 2, :, :, 0, :],
                    rows[:, m % GATHER_RING, :, :].rearrange("p b (f e) -> p b f e", f=2),
                    ACT.Copy,
                ).then_inc(e_hi_made, 1)

            def copy_turned(m):
                act.wait_ge(turn_done, 3 * m + 1)
                if m - PARTNER_RING >= 1:
                    act.wait_ge(multiply_done, LAST_OF_COUPLE[m - PARTNER_RING] + 1)
                nc.scalar.activation(
                    partner[:, m % PARTNER_RING, :], turned[:, (3 * m) % 2, :], ACT.Copy
                ).then_inc(turn_copied, 1)
                for f in (0, 1):
                    act.wait_ge(turn_done, 3 * m + 2 + f)
                    nc.scalar.activation(
                        moving[:, 2 * m + f, :], turned[:, (3 * m + 1 + f) % 2, :], ACT.Copy
                    ).then_inc(turn_copied, 1)

            def copy_odd(m):
                q = m // 2
                act.wait_ge(turn_copied, 3 * m + 1)
                if q >= 2:
                    act.wait_ge(multiply_done, DIAGONAL[q // 2 - 1] + 1)
                for half, source in ((0, m - 1), (1, m)):
                    nc.scalar.activation(
                        odd[half * EMBED : (half + 1) * EMBED, q % 2, :],
                        partner[EMBED:P, source % PARTNER_RING, :],
                        ACT.Copy,
                    ).then_inc(odd_made, 1)

            def copy_z(t):
                last_batch = min(BATCHES, Z_TILE_STEPS * (t + 1))
                act.wait_ge(reduce_done, last_batch)
                if t < Z_TILES - 1:
                    nc.scalar.activation(z[:, t, :], z_sum[:, t % 2, :], ACT.Copy).then_inc(z_copied, 1)
                else:
                    for quadrant in range(COL_TILES):
                        used = slice(32 * quadrant, 32 * quadrant + 2 * LAST_STEPS)
                        last = nc.scalar.activation(z[used, t, :], z_sum[used, t % 2, :], ACT.Copy)
                    last.then_inc(z_copied, 1)

            for g in range(N_GROUPS):
                for c in CHUNK_AT[g]:
                    split_weights_hi(c)
                for m in COUPLE_AT[g]:
                    split_rows_hi(m)
                    copy_turned(m)
                    if m % 2 == 1:
                        copy_odd(m)
                for t in range(Z_TILES - 1):
                    if g == 2 * (Z_TILE_STEPS * (t + 1) - 1) + 5:
                        copy_z(t)
            copy_z(Z_TILES - 1)

            act.wait_ge(mlp_loaded, 16 * (5 + COL_TILES))
            for n in range(0, HIDDEN1 // P, 2):
                act.wait_ge(h1_summed, n + 1)
                nc.scalar.activation(
                    h1[:, n, :], projected[:, n // 2, n % 2, :], ACT.Relu, bias=b1_sb[:, n : n + 1]
                ).then_inc(h1_made, 1)
            act.wait_ge(h2_summed, 1)
            nc.scalar.activation(h2[:, 0, :], turned[:, 0, :], ACT.Relu, bias=b2_sb[:, 0:1]).then_inc(h2_made, 1)

        @block.vector
        def _(dve):
            nc.vector.memset(selector[:], 0.0).then_inc(selector_zeroed, 1)
            dve.wait_ge(selector_zeroed, 1)
            flat = selector[:].rearrange("p k r -> p (k r)")
            nc.vector.memset(flat[0:EMBED, 0 :: 34][:, 0:Z_TILE_STEPS], 1.0).then_inc(selector_made, 1)
            nc.vector.memset(flat[EMBED:P, 1 :: 34][:, 0:Z_TILE_STEPS], 1.0).then_inc(selector_made, 1)

            def split_weights_lo(c):
                dve.wait_ge(w_hi_made, c + 1)
                if c >= SPLIT_RING:
                    dve.wait_ge(project_done, CHUNK_LAST[c - SPLIT_RING] + 1)
                nc.vector.tensor_tensor(
                    w_lo[:, c % SPLIT_RING, :, :].rearrange("p s c -> p (s c)"),
                    w_raw[:, c % RAW_RING, :],
                    w_hi[:, c % SPLIT_RING, :, :].rearrange("p s c -> p (s c)").bitcast(fp32),
                    ALU.subtract,
                ).then_inc(w_lo_made, 1)

            def split_rows_lo(m):
                dve.wait_ge(e_hi_made, m + 1)
                nc.vector.tensor_tensor(
                    parts[:, m % 2, :, :, 1, :],
                    rows[:, m % GATHER_RING, :, :].rearrange("p b (f e) -> p b f e", f=2),
                    parts[:, m % 2, :, :, 0, :].bitcast(fp32),
                    ALU.subtract,
                ).then_inc(e_lo_made, 1)

            def multiply(g):
                m = GROUPS[g][0]
                if m is not None:
                    dve.wait_ge(turn_copied, 3 * m + 1)
                    factor = partner[:, m % PARTNER_RING : m % PARTNER_RING + 1, :].to_broadcast([P, 2, BATCH])
                else:
                    dve.wait_ge(odd_made, 4 * (DIAGONAL.index(g) + 1))
                    factor = odd[:]
                if g >= PRODUCT_RING:
                    dve.wait_ge(reduce_done, (g - PRODUCT_RING) // 2 + 1)
                dve.wait_ge(project_done, g + 1)
                nc.vector.tensor_tensor(
                    product[:, g % PRODUCT_RING, :, :], projected[:, g % 2, :, :], factor, ALU.mult
                ).then_inc(multiply_done, 1)

            for g in range(N_GROUPS):
                for c in CHUNK_AT[g]:
                    split_weights_lo(c)
                for m in COUPLE_AT[g]:
                    split_rows_lo(m)
                multiply(g)

            dve.wait_ge(mlp_loaded, 16 * (5 + COL_TILES))
            for n in range(1, HIDDEN1 // P, 2):
                dve.wait_ge(h1_summed, n + 1)
                nc.vector.tensor_scalar(
                    h1[:, n, :], projected[:, n // 2, n % 2, :], b1_sb[:, n : n + 1], 0.0, ALU.add, ALU.max
                ).then_inc(h1_made, 1)
            dve.wait_ge(h2_summed, 2)
            nc.vector.tensor_scalar(
                h2[:, 1, :], turned[:, 1, :], b2_sb[:, 1:2], 0.0, ALU.add, ALU.max
            ).then_inc(h2_made, 1)
            dve.wait_ge(y_summed, 1)
            nc.vector.tensor_copy(y[:], z_sum[0:1, 0, :]).then_inc(y_made, 1)

        @block.tensor
        def _(pe):
            def turn_bank(index):
                if index >= 2:
                    pe.wait_ge(turn_copied, index - 1)
                return turned[:, index % 2, :]

            def turn(m):
                pe.wait_ge(*rows_ready(m))
                bank = turn_bank(3 * m)
                for b in range(BLOCKS):
                    last = nc.tensor.transpose(
                        bank[:, b * P : (b + 1) * P], rows[:, m % GATHER_RING, b, :], identity[:]
                    )
                last.then_inc(turn_done, 1)
                pe.wait_ge(e_lo_made, m + 1)
                for f in (0, 1):
                    bank = turn_bank(3 * m + 1 + f)
                    for b in range(BLOCKS):
                        last = nc.tensor.transpose(
                            bank[:, b * P : (b + 1) * P],
                            parts[:, m % 2, b, f, :, :].rearrange("p h e -> p (h e)").bitcast(fp32),
                            identity[:],
                        )
                    last.then_inc(turn_done, 1)

            def project(g):
                m, tiles = GROUPS[g]
                if m is not None and tiles[0][1][0][1] == 2 * m - 2:
                    pe.wait_ge(turn_copied, 3 * m)
                if m is None:
                    pe.wait_ge(turn_copied, 3 * (GROUPS[g - 1][0] + 1))
                pe.wait_ge(w_lo_made, max(slots_of(g)) // CHUNK + 1)
                if g >= 2:
                    pe.wait_ge(multiply_done, g - 1)
                for k, (_, passes) in enumerate(tiles):
                    work = [(w, slot, field) for slot, field in passes for w in (w_hi, w_lo)]
                    for n, (w, slot, field) in enumerate(work):
                        last = nc.tensor.matmul(
                            projected[:, g % 2, k, :],
                            w[:, slot // CHUNK % SPLIT_RING, slot % CHUNK, :],
                            moving[:, field, :],
                            start=(n == 0), stop=(n == len(work) - 1),
                        )
                last.then_inc(project_done, 1)

            def reduce(batch):
                t, step = divmod(batch, Z_TILE_STEPS)
                pe.wait_ge(multiply_done, 2 * batch + 2)
                if step == 0 and t >= 2:
                    pe.wait_ge(z_copied, t - 1)
                end = step == Z_TILE_STEPS - 1 or batch == BATCHES - 1
                for quadrant in range(COL_TILES):
                    tile = COL_TILES * batch + quadrant
                    last = nc.tensor.matmul(
                        z_sum[32 * quadrant : 32 * quadrant + 32, t % 2, :],
                        selector[:, step, :],
                        product[:, tile // 2 % PRODUCT_RING, tile % 2, :],
                        start=(step == 0), stop=end, tile_position=(0, 32 * quadrant),
                    )
                last.then_inc(reduce_done, 1)

            pe.wait_ge(constants_made, 1)
            pe.wait_ge(selector_made, 2)
            for g in range(N_GROUPS):
                for m in COUPLE_AT[g]:
                    turn(m)
                project(g)
                if g % 2 == 1 and g >= 3:
                    reduce((g - 3) // 2)
            reduce(BATCHES - 1)

            pe.wait_ge(z_copied, Z_TILES)
            pe.wait_ge(mlp_loaded, 16 * (5 + COL_TILES))
            for n in range(HIDDEN1 // P):
                for t in range(Z_TILES):
                    last = nc.tensor.matmul(
                        projected[:, n // 2, n % 2, :], w1_sb[:, t, n * P : (n + 1) * P], z[:, t, :],
                        start=(t == 0), stop=(t == Z_TILES - 1),
                    )
                last.then_inc(h1_summed, 1)
            pe.wait_ge(h1_made, HIDDEN1 // P)
            for n in range(HIDDEN2 // P):
                for t in range(HIDDEN1 // P):
                    last = nc.tensor.matmul(
                        turned[:, n, :], w2_sb[:, t, n * P : (n + 1) * P], h1[:, t, :],
                        start=(t == 0), stop=(t == HIDDEN1 // P - 1),
                    )
                last.then_inc(h2_summed, 1)
            pe.wait_ge(h2_made, HIDDEN2 // P)
            for t in range(HIDDEN2 // P):
                last = nc.tensor.matmul(
                    z_sum[0:1, 0, :], w3_sb[:, t : t + 1], h2[:, t, :],
                    start=(t == 0), stop=(t == HIDDEN2 // P - 1),
                )
            last.then_inc(y_summed, 1)


def kernel(**inputs):
    import concourse.bacc as bacc
    from concourse.bass_utils import run_bass_kernel_spmd

    given = {name: np.asarray(a) for name, a in inputs.items()}
    arrays = {}
    arrays["ids"] = np.ascontiguousarray(given["ids"].reshape(BLOCKS, P, FIELDS).transpose(1, 0, 2))
    for f in range(FIELDS):
        arrays[f"tbl_{f}"] = np.ascontiguousarray(given[f"tbl_{f}"])
    w = given["L0_rec_w"]
    padded = np.concatenate([w, np.zeros((1, EMBED, EMBED), w.dtype)]).transpose(1, 0, 2)
    arrays["weights"] = np.ascontiguousarray(padded[:, np.array(SLOTS).ravel(), :]).reshape(EMBED, -1)
    row_of = np.zeros((Z_TILES, P), np.int64)
    for tile in range(N_TILES):
        for half, pair in enumerate(GROUPS[tile // 2][1][tile % 2][0]):
            row_of[z_place(tile, half)] = pair
    for d in range(DENSE):
        row_of[Z_TILES - 1, 32 * (d // FREE_ROWS) + 2 * LAST_STEPS + d % FREE_ROWS] = PAIRS + d
    arrays["w1"] = np.ascontiguousarray(given["W_top1"][row_of.T])
    arrays["w2"] = np.ascontiguousarray(given["W_top2"].reshape(-1, P, HIDDEN2).transpose(1, 0, 2))
    arrays["w3"] = np.ascontiguousarray(given["W_top3"].reshape(-1, P).T)
    arrays["b1"] = np.ascontiguousarray(given["b_top1"].reshape(-1, P).T)
    arrays["b2"] = np.ascontiguousarray(given["b_top2"].reshape(-1, P).T)
    arrays["dense"] = np.ascontiguousarray(given["dense_ctx"].T)

    nc = bacc.Bacc("TRN2", target_bir_lowering=False, num_devices=1)
    aps = {
        name: nc.dram_tensor(f"in_{name}", a.shape, mybir.dt.from_np(a.dtype), kind="ExternalInput").ap()
        for name, a in arrays.items()
    }
    out = nc.dram_tensor("out_y", (1, BATCH), mybir.dt.float32, kind="ExternalOutput").ap()
    build_tower(
        nc, aps["ids"], [aps[f"tbl_{f}"] for f in range(FIELDS)], aps["weights"], aps["w1"], aps["b1"],
        aps["w2"], aps["b2"], aps["w3"], aps["dense"], out,
    )
    result = run_bass_kernel_spmd(nc, [{f"in_{name}": a for name, a in arrays.items()}], core_ids=[0])
    return result.results[0]["out_y"].reshape(BATCH, 1)
```

```python
from contextlib import ExitStack

import concourse.bass as bass
import numpy as np
from concourse import mybir

FIELDS = 32
EMBED = 64
BATCH = 512
DENSE = 16
HIDDEN1 = 512
HIDDEN2 = 256
P = 128
BLOCKS = BATCH // P
COUPLES = FIELDS // 2
PAIRS = FIELDS * (FIELDS - 1) // 2

CHUNK = 8
CHUNK_COLS = CHUNK * P
RAW_RING = 3
SPLIT_RING = 7
PRODUCT_RING = 4
GATHER_RING = 4
PARTNER_RING = 3
PROJECT_RING = 3
GPSIMD_FROM = 19
WEIGHT_LEAD = 18


def pair_index(i, j):
    return i * (FIELDS - 1) - i * (i - 1) // 2 + (j - i - 1)


def build_plan():
    groups, slots, first_group = [], [], {}
    for m in range(COUPLES):
        first_group[m] = len(groups)
        for i in range(0, 2 * m, 2):
            tiles = []
            for field in (i, i + 1):
                halves = (pair_index(field, 2 * m), pair_index(field, 2 * m + 1))
                tiles.append((halves, [(len(slots), field)]))
                slots.append(halves)
            groups.append((m, tiles))
        if m % 4 == 3:
            tiles = []
            for q in (m // 2 - 1, m // 2):
                halves = (pair_index(4 * q, 4 * q + 1), pair_index(4 * q + 2, 4 * q + 3))
                tiles.append((halves, [(len(slots), 4 * q), (len(slots) + 1, 4 * q + 2)]))
                slots += [(halves[0], PAIRS), (PAIRS, halves[1])]
            groups.append((None, tiles))
    return groups, slots, first_group


GROUPS, SLOTS, FIRST_GROUP = build_plan()
N_GROUPS = len(GROUPS)
N_CHUNKS = len(SLOTS) // CHUNK
N_TILES = 2 * N_GROUPS
COL_TILES = 4
Z_TILE_STEPS = 16
BATCHES = N_TILES // COL_TILES
Z_TILES = -(-BATCHES // Z_TILE_STEPS)
LAST_STEPS = BATCHES - (Z_TILES - 1) * Z_TILE_STEPS
FREE_ROWS = 32 - 2 * LAST_STEPS


def z_place(tile, half):
    batch, quadrant = divmod(tile, COL_TILES)
    return batch // Z_TILE_STEPS, 32 * quadrant + 2 * (batch % Z_TILE_STEPS) + half


def slots_of(group):
    return [slot for _, passes in GROUPS[group][1] for slot, _ in passes]


CHUNK_FIRST = [min(g for g in range(N_GROUPS) if c in [s // CHUNK for s in slots_of(g)]) for c in range(N_CHUNKS)]
CHUNK_LAST = [max(g for g in range(N_GROUPS) if c in [s // CHUNK for s in slots_of(g)]) for c in range(N_CHUNKS)]


def couple_step(m):
    if m <= 1:
        return 0
    return FIRST_GROUP[m] - (0 if m <= 6 else 2)


def moving_steps(m):
    return (min(FIRST_GROUP[m], N_GROUPS - 1), min(FIRST_GROUP[m] + 1, LAST_OF_COUPLE[m]))


LAST_OF_COUPLE = {m: max(g for g in range(N_GROUPS) if GROUPS[g][0] == m) for m in range(1, COUPLES)}
COUPLE_AT = {g: [m for m in range(COUPLES) if couple_step(m) == g] for g in range(N_GROUPS)}
MOVING_AT = {
    g: [(m, f) for m in range(1, COUPLES) for f in (0, 1) if moving_steps(m)[f] == g and 2 * m + f < FIELDS - 1]
    for g in range(N_GROUPS)
}
CHUNK_AT = {g: [c for c in range(N_CHUNKS) if max(0, CHUNK_FIRST[c] - WEIGHT_LEAD) == g] for g in range(N_GROUPS)}
DIAGONAL = [g for g in range(N_GROUPS) if GROUPS[g][0] is None]


def build_tower(nc, ids, tables, weights, w1, b1, w2, b2, w3, dense, out):
    fp32 = mybir.dt.float32
    fp32r = mybir.dt.float32r
    int32 = mybir.dt.int32
    ALU = mybir.AluOpType
    ACT = mybir.ActivationFunctionType

    ctx = ExitStack()
    with ctx:

        def sb(name, shape, dt=fp32):
            return ctx.enter_context(nc.sbuf_tensor(name, shape, dt))

        def pb(name, shape):
            return ctx.enter_context(nc.psum_tensor(name, shape, fp32))

        def sem(name):
            return ctx.enter_context(nc.semaphore(name))

        ids_sb = sb("ids_sb", [P, BLOCKS, FIELDS], int32)
        rows = sb("rows", [P, GATHER_RING, BLOCKS, 2 * EMBED])
        parts = sb("parts", [P, 2, BLOCKS, 2, 2, EMBED], fp32r)
        moving = sb("moving", [P, FIELDS - 1, BATCH], fp32r)
        partner = sb("partner", [P, PARTNER_RING, BATCH])
        odd = sb("odd", [P, 2, BATCH])
        w_raw = sb("w_raw", [P, RAW_RING, CHUNK_COLS])
        layers = w_raw[:].rearrange("p r (h b) -> p (r h) b", b=BATCH)
        w_hi = sb("w_hi", [P, SPLIT_RING, CHUNK, P], fp32r)
        w_lo = sb("w_lo", [P, SPLIT_RING, CHUNK, P], fp32r)
        product = sb("product", [P, PRODUCT_RING, 2, BATCH])
        selector = sb("selector", [P, Z_TILE_STEPS, 32])
        identity = sb("identity", [P, P])
        z = sb("z", [P, Z_TILES, BATCH])
        w1_sb = sb("w1_sb", [P, Z_TILES, HIDDEN1])
        w2_sb = sb("w2_sb", [P, HIDDEN1 // P, HIDDEN2])
        w3_sb = sb("w3_sb", [P, HIDDEN2 // P])
        b1_sb = sb("b1_sb", [P, HIDDEN1 // P])
        b2_sb = sb("b2_sb", [P, HIDDEN2 // P])
        h1 = layers[:, 0 : HIDDEN1 // P, :]
        h2 = layers[:, HIDDEN1 // P : (HIDDEN1 + HIDDEN2) // P, :]
        y = sb("y", [1, BATCH])

        projected = pb("projected", [P, PROJECT_RING, 2, BATCH])
        turned = pb("turned", [P, BATCH])
        z_sum = pb("z_sum", [P, BATCH])
        spare = projected[:].rearrange("p r k b -> p (r k) b")

        ids_loaded = sem("ids_loaded")
        mlp_loaded = sem("mlp_loaded")
        rows_gathered = [sem(f"rows_gathered_{k}") for k in range(GATHER_RING)]
        w_loaded = [sem(f"w_loaded_{k}") for k in range(RAW_RING)]
        zeroed = sem("zeroed")
        constants_made = sem("constants_made")
        selector_zeroed = sem("selector_zeroed")
        selector_made = sem("selector_made")
        w_hi_made = sem("w_hi_made")
        w_lo_made = sem("w_lo_made")
        e_hi_made = sem("e_hi_made")
        e_lo_made = sem("e_lo_made")
        turn_done = sem("turn_done")
        turn_copied = sem("turn_copied")
        odd_made = sem("odd_made")
        project_done = sem("project_done")
        multiply_done = sem("multiply_done")
        reduce_done = sem("reduce_done")
        z_copied = sem("z_copied")
        h1_summed = sem("h1_summed")
        h1_made = sem("h1_made")
        h2_summed = sem("h2_summed")
        h2_made = sem("h2_made")
        y_summed = sem("y_summed")
        y_made = sem("y_made")
        y_stored = sem("y_stored")

        def rows_ready(m):
            return rows_gathered[m % GATHER_RING], 16 * 2 * BLOCKS * (m // GATHER_RING + 1)

        def raw_ready(c):
            return w_loaded[c % RAW_RING], 32 * (c // RAW_RING + 1)

        block = ctx.enter_context(nc.Block())

        @block.sync
        def _(sp):
            sp.dma_start(ids_sb[:], ids).then_inc(ids_loaded, 16)
            for c in range(N_CHUNKS):
                if c >= RAW_RING:
                    sp.wait_ge(w_hi_made, c - RAW_RING + 1)
                    sp.wait_ge(w_lo_made, c - RAW_RING + 1)
                for half in (0, 1):
                    sp.dma_start(
                        w_raw[half * EMBED : (half + 1) * EMBED, c % RAW_RING, :],
                        weights[:, c * CHUNK_COLS : (c + 1) * CHUNK_COLS],
                    ).then_inc(w_loaded[c % RAW_RING], 16)
                if c == 6:
                    sp.dma_start(w1_sb[:], w1).then_inc(mlp_loaded, 16)
                    sp.dma_start(w2_sb[:], w2).then_inc(mlp_loaded, 16)
                    sp.dma_start(w3_sb[:], w3).then_inc(mlp_loaded, 16)
                    sp.dma_start(b1_sb[:], b1).then_inc(mlp_loaded, 16)
                    sp.dma_start(b2_sb[:], b2).then_inc(mlp_loaded, 16)
                    for quadrant in range(COL_TILES):
                        row = 32 * quadrant + 2 * LAST_STEPS
                        sp.dma_start(
                            z[row : row + FREE_ROWS, Z_TILES - 1, :],
                            dense[quadrant * FREE_ROWS : (quadrant + 1) * FREE_ROWS, :],
                        ).then_inc(mlp_loaded, 16)
            sp.wait_ge(y_made, 1)
            sp.dma_start(out, y[:]).then_inc(y_stored, 16)
            sp.wait_ge(y_stored, 16)

        @block.gpsimd
        def _(pool):
            pool.memset(identity[:], 0.0).then_inc(zeroed, 1)
            pool.wait_ge(zeroed, 1)
            nc.gpsimd.affine_select(
                out=identity[:], in_=identity[:], compare_op=ALU.not_equal, fill=1.0,
                base=0, pattern=[[-1, P]], channel_multiplier=1,
            ).then_inc(constants_made, 1)
            pool.wait_ge(ids_loaded, 16)
            for m in range(COUPLES):
                if m >= GATHER_RING:
                    pool.wait_ge(e_hi_made, m - GATHER_RING + 1)
                    pool.wait_ge(e_lo_made, m - GATHER_RING + 1)
                    pool.wait_ge(turn_done, 3 * (m - GATHER_RING) + 1)
                for field in (2 * m, 2 * m + 1):
                    for b in range(BLOCKS):
                        col = (field % 2) * EMBED
                        nc.gpsimd.indirect_dma_start(
                            rows[:, m % GATHER_RING, b, col : col + EMBED], None,
                            tables[field],
                            bass.IndirectOffsetOnAxis(ap=ids_sb[:, b, field : field + 1], axis=0),
                        ).then_inc(rows_gathered[m % GATHER_RING], 16)

            for c in range(GPSIMD_FROM, N_CHUNKS):
                pool.wait_ge(w_hi_made, c + 1)
                pool.wait_ge(project_done, CHUNK_LAST[c - SPLIT_RING] + 1)
                if c == GPSIMD_FROM:
                    pool.wait_ge(w_lo_made, c)
                nc.gpsimd.tensor_tensor(
                    w_lo[:, c % SPLIT_RING, :, :].rearrange("p s c -> p (s c)"),
                    w_raw[:, c % RAW_RING, :],
                    w_hi[:, c % SPLIT_RING, :, :].rearrange("p s c -> p (s c)").bitcast(fp32),
                    ALU.subtract,
                ).then_inc(w_lo_made, 1)

        @block.scalar
        def _(act):
            def split_weights_hi(c):
                act.wait_ge(*raw_ready(c))
                if c >= SPLIT_RING:
                    act.wait_ge(project_done, CHUNK_LAST[c - SPLIT_RING] + 1)
                nc.scalar.activation(
                    w_hi[:, c % SPLIT_RING, :, :].rearrange("p s c -> p (s c)"), w_raw[:, c % RAW_RING, :], ACT.Copy
                ).then_inc(w_hi_made, 1)

            def split_rows_hi(m):
                act.wait_ge(*rows_ready(m))
                if m >= 2:
                    act.wait_ge(turn_done, 3 * (m - 2) + 3)
                nc.scalar.activation(
                    parts[:, m % 2, :, :, 0, :],
                    rows[:, m % GATHER_RING, :, :].rearrange("p b (f e) -> p b f e", f=2),
                    ACT.Copy,
                ).then_inc(e_hi_made, 1)

            def copy_partner(m):
                act.wait_ge(turn_done, 3 * m + 1)
                if m - PARTNER_RING >= 1:
                    act.wait_ge(multiply_done, LAST_OF_COUPLE[m - PARTNER_RING] + 1)
                nc.scalar.activation(
                    partner[:, m % PARTNER_RING, :], turned[:], ACT.Copy
                ).then_inc(turn_copied, 1)

            def copy_moving(m, f):
                act.wait_ge(turn_done, 3 * m + 2 + f)
                nc.scalar.activation(moving[:, 2 * m + f, :], turned[:], ACT.Copy).then_inc(turn_copied, 1)

            def copy_odd(m):
                q = m // 2
                act.wait_ge(turn_copied, 3 * m + 1)
                if q >= 2:
                    act.wait_ge(multiply_done, DIAGONAL[q // 2 - 1] + 1)
                for half, source in ((0, m - 1), (1, m)):
                    nc.scalar.activation(
                        odd[half * EMBED : (half + 1) * EMBED, q % 2, :],
                        partner[EMBED:P, source % PARTNER_RING, :],
                        ACT.Copy,
                    ).then_inc(odd_made, 1)

            def copy_z(t):
                last_batch = min(BATCHES, Z_TILE_STEPS * (t + 1))
                act.wait_ge(reduce_done, last_batch)
                if t < Z_TILES - 1:
                    nc.scalar.activation(z[:, t, :], z_sum[:], ACT.Copy).then_inc(z_copied, 1)
                else:
                    for quadrant in range(COL_TILES):
                        used = slice(32 * quadrant, 32 * quadrant + 2 * LAST_STEPS)
                        last = nc.scalar.activation(z[used, t, :], z_sum[used, :], ACT.Copy)
                    last.then_inc(z_copied, 1)

            for g in range(N_GROUPS):
                for c in CHUNK_AT[g]:
                    split_weights_hi(c)
                for m in COUPLE_AT[g]:
                    split_rows_hi(m)
                    copy_partner(m)
                    if m == 0:
                        copy_moving(0, 0)
                        copy_moving(0, 1)
                    if m % 2 == 1:
                        copy_odd(m)
                for m, f in MOVING_AT[g]:
                    copy_moving(m, f)
                for t in range(Z_TILES - 1):
                    if g == 2 * (Z_TILE_STEPS * (t + 1) - 1) + 3:
                        copy_z(t)
            copy_z(Z_TILES - 1)

            act.wait_ge(mlp_loaded, 16 * (5 + COL_TILES))
            for n in range(0, HIDDEN1 // P, 2):
                act.wait_ge(h1_summed, n + 1)
                nc.scalar.activation(
                    h1[:, n, :], spare[:, n, :], ACT.Relu, bias=b1_sb[:, n : n + 1]
                ).then_inc(h1_made, 1)
            act.wait_ge(h2_summed, 1)
            nc.scalar.activation(h2[:, 0, :], spare[:, HIDDEN1 // P, :], ACT.Relu, bias=b2_sb[:, 0:1]).then_inc(h2_made, 1)

        @block.vector
        def _(dve):
            nc.vector.memset(selector[:], 0.0).then_inc(selector_zeroed, 1)
            dve.wait_ge(selector_zeroed, 1)
            flat = selector[:].rearrange("p k r -> p (k r)")
            nc.vector.memset(flat[0:EMBED, 0 :: 34][:, 0:Z_TILE_STEPS], 1.0).then_inc(selector_made, 1)
            nc.vector.memset(flat[EMBED:P, 1 :: 34][:, 0:Z_TILE_STEPS], 1.0).then_inc(selector_made, 1)

            def split_weights_lo(c):
                dve.wait_ge(w_hi_made, c + 1)
                if c >= SPLIT_RING:
                    dve.wait_ge(project_done, CHUNK_LAST[c - SPLIT_RING] + 1)
                nc.vector.tensor_tensor(
                    w_lo[:, c % SPLIT_RING, :, :].rearrange("p s c -> p (s c)"),
                    w_raw[:, c % RAW_RING, :],
                    w_hi[:, c % SPLIT_RING, :, :].rearrange("p s c -> p (s c)").bitcast(fp32),
                    ALU.subtract,
                ).then_inc(w_lo_made, 1)

            def split_rows_lo(m):
                dve.wait_ge(e_hi_made, m + 1)
                nc.vector.tensor_tensor(
                    parts[:, m % 2, :, :, 1, :],
                    rows[:, m % GATHER_RING, :, :].rearrange("p b (f e) -> p b f e", f=2),
                    parts[:, m % 2, :, :, 0, :].bitcast(fp32),
                    ALU.subtract,
                ).then_inc(e_lo_made, 1)

            def multiply(g):
                m = GROUPS[g][0]
                if m is not None:
                    dve.wait_ge(turn_copied, 3 * m + 1)
                    factor = partner[:, m % PARTNER_RING : m % PARTNER_RING + 1, :].to_broadcast([P, 2, BATCH])
                else:
                    dve.wait_ge(odd_made, 4 * (DIAGONAL.index(g) + 1))
                    factor = odd[:]
                if g >= PRODUCT_RING:
                    dve.wait_ge(reduce_done, (g - PRODUCT_RING) // 2 + 1)
                dve.wait_ge(project_done, g + 1)
                nc.vector.tensor_tensor(
                    product[:, g % PRODUCT_RING, :, :], projected[:, g % PROJECT_RING, :, :], factor, ALU.mult
                ).then_inc(multiply_done, 1)

            for g in range(N_GROUPS):
                for c in CHUNK_AT[g]:
                    if c < GPSIMD_FROM:
                        split_weights_lo(c)
                for m in COUPLE_AT[g]:
                    split_rows_lo(m)
                multiply(g)

            dve.wait_ge(mlp_loaded, 16 * (5 + COL_TILES))
            for n in range(1, HIDDEN1 // P, 2):
                dve.wait_ge(h1_summed, n + 1)
                nc.vector.tensor_scalar(
                    h1[:, n, :], spare[:, n, :], b1_sb[:, n : n + 1], 0.0, ALU.add, ALU.max
                ).then_inc(h1_made, 1)
            dve.wait_ge(h2_summed, 2)
            nc.vector.tensor_scalar(
                h2[:, 1, :], spare[:, HIDDEN1 // P + 1, :], b2_sb[:, 1:2], 0.0, ALU.add, ALU.max
            ).then_inc(h2_made, 1)
            dve.wait_ge(y_summed, 1)
            nc.vector.tensor_copy(y[:], turned[0:1, :]).then_inc(y_made, 1)

        @block.tensor
        def _(pe):
            def turn(index, blocks):
                if index >= 1:
                    pe.wait_ge(turn_copied, index)
                for b, rows_of_block in enumerate(blocks):
                    last = nc.tensor.transpose(turned[:, b * P : (b + 1) * P], rows_of_block, identity[:])
                last.then_inc(turn_done, 1)

            def turn_partner(m):
                pe.wait_ge(*rows_ready(m))
                turn(3 * m, [rows[:, m % GATHER_RING, b, :] for b in range(BLOCKS)])

            def turn_moving(m, f):
                pe.wait_ge(e_lo_made, m + 1)
                both = parts[:, m % 2, :, f, :, :].rearrange("p b h e -> p b (h e)").bitcast(fp32)
                turn(3 * m + 1 + f, [both[:, b, :] for b in range(BLOCKS)])

            def project(g):
                m, tiles = GROUPS[g]
                if m is not None and tiles[0][1][0][1] == 2 * m - 2:
                    pe.wait_ge(turn_copied, 3 * m)
                if m is None:
                    pe.wait_ge(turn_copied, 3 * GROUPS[g - 1][0] + 2)
                pe.wait_ge(w_lo_made, max(slots_of(g)) // CHUNK + 1)
                if g >= PROJECT_RING:
                    pe.wait_ge(multiply_done, g - PROJECT_RING + 1)
                for k, (_, passes) in enumerate(tiles):
                    work = [(w, slot, field) for slot, field in passes for w in (w_hi, w_lo)]
                    for n, (w, slot, field) in enumerate(work):
                        last = nc.tensor.matmul(
                            projected[:, g % PROJECT_RING, k, :],
                            w[:, slot // CHUNK % SPLIT_RING, slot % CHUNK, :],
                            moving[:, field, :],
                            start=(n == 0), stop=(n == len(work) - 1),
                        )
                last.then_inc(project_done, 1)

            def reduce(batch):
                t, step = divmod(batch, Z_TILE_STEPS)
                pe.wait_ge(multiply_done, 2 * batch + 2)
                if step == 0 and t >= 1:
                    pe.wait_ge(z_copied, t)
                end = step == Z_TILE_STEPS - 1 or batch == BATCHES - 1
                for quadrant in range(COL_TILES):
                    tile = COL_TILES * batch + quadrant
                    last = nc.tensor.matmul(
                        z_sum[32 * quadrant : 32 * quadrant + 32, :],
                        selector[:, step, :],
                        product[:, tile // 2 % PRODUCT_RING, tile % 2, :],
                        start=(step == 0), stop=end, tile_position=(0, 32 * quadrant),
                    )
                last.then_inc(reduce_done, 1)

            pe.wait_ge(constants_made, 1)
            pe.wait_ge(selector_made, 2)
            for g in range(N_GROUPS):
                for m in COUPLE_AT[g]:
                    turn_partner(m)
                    if m == 0:
                        turn_moving(0, 0)
                        turn_moving(0, 1)
                project(g)
                for m, f in MOVING_AT[g]:
                    turn_moving(m, f)
                if g % 2 == 1 and g >= 3:
                    reduce((g - 3) // 2)
            reduce(BATCHES - 1)

            pe.wait_ge(z_copied, Z_TILES)
            pe.wait_ge(mlp_loaded, 16 * (5 + COL_TILES))
            for n in range(HIDDEN1 // P):
                for t in range(Z_TILES):
                    last = nc.tensor.matmul(
                        spare[:, n, :], w1_sb[:, t, n * P : (n + 1) * P], z[:, t, :],
                        start=(t == 0), stop=(t == Z_TILES - 1),
                    )
                last.then_inc(h1_summed, 1)
            pe.wait_ge(h1_made, HIDDEN1 // P)
            for n in range(HIDDEN2 // P):
                for t in range(HIDDEN1 // P):
                    last = nc.tensor.matmul(
                        spare[:, HIDDEN1 // P + n, :], w2_sb[:, t, n * P : (n + 1) * P], h1[:, t, :],
                        start=(t == 0), stop=(t == HIDDEN1 // P - 1),
                    )
                last.then_inc(h2_summed, 1)
            pe.wait_ge(h2_made, HIDDEN2 // P)
            for t in range(HIDDEN2 // P):
                last = nc.tensor.matmul(
                    turned[0:1, :], w3_sb[:, t : t + 1], h2[:, t, :],
                    start=(t == 0), stop=(t == HIDDEN2 // P - 1),
                )
            last.then_inc(y_summed, 1)


def kernel(**inputs):
    import concourse.bacc as bacc
    from concourse.bass_utils import run_bass_kernel_spmd

    given = {name: np.asarray(a) for name, a in inputs.items()}
    arrays = {}
    arrays["ids"] = np.ascontiguousarray(given["ids"].reshape(BLOCKS, P, FIELDS).transpose(1, 0, 2))
    for f in range(FIELDS):
        arrays[f"tbl_{f}"] = np.ascontiguousarray(given[f"tbl_{f}"])
    w = given["L0_rec_w"]
    padded = np.concatenate([w, np.zeros((1, EMBED, EMBED), w.dtype)]).transpose(1, 0, 2)
    arrays["weights"] = np.ascontiguousarray(padded[:, np.array(SLOTS).ravel(), :]).reshape(EMBED, -1)
    row_of = np.zeros((Z_TILES, P), np.int64)
    for tile in range(N_TILES):
        for half, pair in enumerate(GROUPS[tile // 2][1][tile % 2][0]):
            row_of[z_place(tile, half)] = pair
    for d in range(DENSE):
        row_of[Z_TILES - 1, 32 * (d // FREE_ROWS) + 2 * LAST_STEPS + d % FREE_ROWS] = PAIRS + d
    arrays["w1"] = np.ascontiguousarray(given["W_top1"][row_of.T])
    arrays["w2"] = np.ascontiguousarray(given["W_top2"].reshape(-1, P, HIDDEN2).transpose(1, 0, 2))
    arrays["w3"] = np.ascontiguousarray(given["W_top3"].reshape(-1, P).T)
    arrays["b1"] = np.ascontiguousarray(given["b_top1"].reshape(-1, P).T)
    arrays["b2"] = np.ascontiguousarray(given["b_top2"].reshape(-1, P).T)
    arrays["dense"] = np.ascontiguousarray(given["dense_ctx"].T)

    nc = bacc.Bacc("TRN2", target_bir_lowering=False, num_devices=1)
    aps = {
        name: nc.dram_tensor(f"in_{name}", a.shape, mybir.dt.from_np(a.dtype), kind="ExternalInput").ap()
        for name, a in arrays.items()
    }
    out = nc.dram_tensor("out_y", (1, BATCH), mybir.dt.float32, kind="ExternalOutput").ap()
    build_tower(
        nc, aps["ids"], [aps[f"tbl_{f}"] for f in range(FIELDS)], aps["weights"], aps["w1"], aps["b1"],
        aps["w2"], aps["b2"], aps["w3"], aps["dense"], out,
    )
    result = run_bass_kernel_spmd(nc, [{f"in_{name}": a for name, a in arrays.items()}], core_ids=[0])
    return result.results[0]["out_y"].reshape(BATCH, 1)
```

```python
from contextlib import ExitStack

import concourse.bass as bass
import numpy as np
from concourse import mybir

FIELDS = 32
EMBED = 64
BATCH = 512
DENSE = 16
HIDDEN1 = 512
HIDDEN2 = 256
P = 128
BLOCKS = BATCH // P
COUPLES = FIELDS // 2
PAIRS = FIELDS * (FIELDS - 1) // 2

HOT_ROWS = 1000
HOT_K = 125
HOT_STEPS = HOT_ROWS // HOT_K
HOT_COUPLES = [0, 3]
GATHERED = [m for m in range(COUPLES) if m not in HOT_COUPLES]
HOT_PLACES = [2 * m + f for m in HOT_COUPLES for f in (0, 1)]
HOT_FIELDS = len(HOT_PLACES)
HOT_CHOICE = [0, 1, 4, 6]
FIELD_AT = [f for f in range(FIELDS) if f not in HOT_CHOICE]
for _place, _field in zip(HOT_PLACES, HOT_CHOICE):
    FIELD_AT.insert(_place, _field)

CHUNK = 8
CHUNK_COLS = CHUNK * P
RAW_RING = 3
SPLIT_RING = 7
CHUNK_LEAD = [
    7, 6, 8, 10, 12, 14, 16, 15, 18, 17, 18, 18, 18, 18, 18,
    18, 17, 17, 17, 18, 18, 18, 18, 17, 16, 18, 18, 16, 20,
]
COUPLE_LEAD = {
    2: (0, -1, -1, -1),
    3: (0, 0, 0, -2),
    4: (2, 0, 0, 0),
    5: (2, 2, 0, -1),
    6: (2, 2, 0, -1),
    7: (2, 2, 1, -1),
    8: (2, 2, 0, -1),
    9: (6, None, 5, 3),
    10: (6, None, 5, 3),
    11: (7, None, 5, 3),
    12: (6, None, 5, 3),
    13: (6, None, 4, 2),
    14: (6, None, 5, 3),
    15: (7, None, 5, 3),
}
GPSIMD_CHUNKS = {6: 11, 9: 14, 11: 16, 13: 19, 15: 20, 17: 23, 18: 24, 19: 24, 20: 25}
GPSIMD_CHUNKS.update({c: FIELDS - HOT_FIELDS for c in range(max(GPSIMD_CHUNKS) + 1, PAIRS // 2 // CHUNK)})
PRODUCT_RING = 4
PROJECT_RING = 3
GATHER_RING = 4
ADD_FROM = min(m for m, lead in COUPLE_LEAD.items() if lead[1] is None)
PARTNER_RING = 3
ODD_SLOTS = (PARTNER_RING, PARTNER_RING + 1)
WARM_UPS = 22
COL_TILES = 4
Z_TILE_STEPS = 16


def pair_index(i, j):
    return i * (FIELDS - 1) - i * (i - 1) // 2 + (j - i - 1)


def build_plan():
    tiles, first_tile = [], {}
    for quad in range(FIELDS // 4):
        a, b, c, d = range(4 * quad, 4 * quad + 4)
        for m in (2 * quad, 2 * quad + 1):
            first_tile[m] = len(tiles)
            tiles += [(i, (2 * m, 2 * m + 1), m % PARTNER_RING, m) for i in range(a)]
        tiles.append((b, (c, d), m % PARTNER_RING, m))
        tiles.append((a, (b, c), ODD_SLOTS[0], quad))
        tiles.append((d, (a, c), ODD_SLOTS[1], quad))
    groups = [sorted(tiles[n : n + 2], key=lambda tile: tile[2]) for n in range(0, len(tiles), 2)]
    return groups, {m: n // 2 for m, n in first_tile.items()}


GROUPS, FIRST_GROUP = build_plan()
TILES = [tile for group in GROUPS for tile in group]
N_GROUPS = len(GROUPS)
N_TILES = len(TILES)
N_CHUNKS = N_TILES // CHUNK
GROUPS_PER_CHUNK = CHUNK // 2
BATCHES = N_TILES // COL_TILES
Z_TILES = -(-BATCHES // Z_TILE_STEPS)
LAST_STEPS = BATCHES - (Z_TILES - 1) * Z_TILE_STEPS
FREE_ROWS = 32 - 2 * LAST_STEPS


def is_odd(tile):
    return tile[2] in ODD_SLOTS


def last_group(odd, number):
    found = [g for g, group in enumerate(GROUPS) for t in group if is_odd(t) == odd and t[3] == number]
    return max(found, default=-1)


def last_projected(place):
    return max(g for g, group in enumerate(GROUPS) for tile in group if tile[0] == place)


def z_place(tile, half):
    batch, quadrant = divmod(tile, COL_TILES)
    return batch // Z_TILE_STEPS, 32 * quadrant + 2 * (batch % Z_TILE_STEPS) + half


def coming(m, step):
    return FIRST_GROUP[m] - COUPLE_LEAD[m][step]


PARTNER_AT = {g: [m for m in range(2, ADD_FROM) if coming(m, 1) == g] for g in range(N_GROUPS)}
SPLIT_AT = {g: [m for m in GATHERED[1:] if coming(m, 0) == g] for g in range(N_GROUPS)}
ODD_AT = {g: [m // 2 for m in range(3, COUPLES, 2) if FIRST_GROUP[m] == g] for g in range(N_GROUPS)}
HOT_AT = {g: {1: [1]}.get(g, []) for g in range(N_GROUPS)}
MOVING_AT = {g: [(m, f) for m in GATHERED[1:] for f in (0, 1) if coming(m, 2 + f) == g] for g in range(N_GROUPS)}
TURNS = [(m, what) for m, what in ((0, 0), (0, 1), (0, "partner"), (1, "partner"), (1, 0), (1, 1))]
for _g in range(N_GROUPS):
    TURNS += [(HOT_COUPLES[q], f) for q in HOT_AT[_g] for f in (0, 1)]
    TURNS += [(m, "partner") for m in PARTNER_AT[_g]] + MOVING_AT[_g]


def turn_number(m, what):
    return TURNS.index((m, what)) + 1


def is_look_up(m, what):
    return m in HOT_COUPLES and what != "partner"


def done_number(m, what):
    return sum(not is_look_up(*turn) for turn in TURNS[: turn_number(m, what)])


EARLY_TURNS = sum(1 for g in range(4) for _ in HOT_AT[g] + PARTNER_AT[g] + MOVING_AT[g]) + 6


def in_z_bank(number):
    return number <= EARLY_TURNS and number % 2 == 0


def bank_free_at(number):
    return max((n for n in range(1, number) if in_z_bank(n) == in_z_bank(number)), default=0)


LAST_IN_Z_BANK = max(n for n in range(1, len(TURNS)) if in_z_bank(n))


def moving_number(place):
    return turn_number(place // 2, place % 2)


CHUNK_AT = {
    g: [c for c in range(2, N_CHUNKS) if c * GROUPS_PER_CHUNK - CHUNK_LEAD[c - 2] == g] for g in range(N_GROUPS)
}


def build_tower(nc, ids, hot_ids, tables, weights, w1, b1, w2, b2, w3, dense, out):
    fp32 = mybir.dt.float32
    fp32r = mybir.dt.float32r
    int32 = mybir.dt.int32
    ALU = mybir.AluOpType
    ACT = mybir.ActivationFunctionType

    ctx = ExitStack()
    with ctx:

        def sb(name, shape, dt=fp32):
            return ctx.enter_context(nc.sbuf_tensor(name, shape, dt))

        def pb(name, shape):
            return ctx.enter_context(nc.psum_tensor(name, shape, fp32))

        def sem(name):
            return ctx.enter_context(nc.semaphore(name))

        ids_sb = sb("ids_sb", [P, BLOCKS, FIELDS], int32)
        rows = sb("rows", [P, GATHER_RING, BLOCKS, 2 * EMBED])
        parts = sb("parts", [P, 2, BLOCKS, 2, 2, EMBED], fp32r)
        moving = sb("moving", [P, FIELDS, BATCH], fp32r)
        factors = sb("factors", [P, PARTNER_RING + 2, BATCH])
        w_raw = sb("w_raw", [P, RAW_RING, CHUNK_COLS])
        w_hi = sb("w_hi", [P, SPLIT_RING, CHUNK_COLS], fp32r)
        w_lo = sb("w_lo", [P, SPLIT_RING, CHUNK_COLS], fp32r)
        product = sb("product", [P, PRODUCT_RING, 2, BATCH])
        selector = sb("selector", [P, Z_TILE_STEPS, 32])
        identity = sb("identity", [P, P])
        identity_r = sb("identity_r", [P, P], fp32r)
        fold = sb("fold", [P, 3 * EMBED], fp32r)
        z = sb("z", [P, Z_TILES, BATCH])
        w1_sb = sb("w1_sb", [P, Z_TILES, HIDDEN1])
        w2_sb = sb("w2_sb", [P, HIDDEN1 // P, HIDDEN2])
        w3_sb = sb("w3_sb", [P, HIDDEN2 // P])
        b1_sb = sb("b1_sb", [P, HIDDEN1 // P])
        b2_sb = sb("b2_sb", [P, HIDDEN2 // P])
        row_number = sb("row_number", [P, HOT_STEPS])
        y = sb("y", [1, BATCH])

        layers = w_raw[:].rearrange("p r (h b) -> p (r h) b", b=BATCH)
        h1 = layers[:, 0 : HIDDEN1 // P, :]
        h2 = layers[:, HIDDEN1 // P : (HIDDEN1 + HIDDEN2) // P, :]

        w1_hi = moving[:, 0:4, :]
        w2_hi = moving[:, 4:6, :].rearrange("p x (k n) -> p (x k) n", n=HIDDEN2)
        z_hi = moving[:, 6:10, :]
        h1_hi = moving[:, 10:14, :]
        assert N_CHUNKS % SPLIT_RING == 3
        w1_lo = w_lo[:, 3:5, :].rearrange("p r (x n) -> p (r x) n", n=HIDDEN1)
        w2_lo = w_lo[:, 5, :].rearrange("p (k n) -> p k n", n=HIDDEN2)
        z_lo = w_hi[:, 3:5, :].rearrange("p r (x b) -> p (r x) b", b=BATCH)
        h1_lo = w_hi[:, 5:7, :].rearrange("p r (x b) -> p (r x) b", b=BATCH)

        hot_number = w1_sb[0:HOT_K, 0:HOT_FIELDS, :]
        hot_id = hot_number.bitcast(int32)
        hot_raw = [w2_sb[0:HOT_K, 0:2, :], w2_sb[0:HOT_K, 2:4, :]]
        hot_raw = [t.rearrange("p x n -> p (x n)") for t in hot_raw] + [z[0:HOT_K, 2, :], z[0:HOT_K, 3, :]]
        hot_parts = moving[0:HOT_K, 12:16, :].rearrange("p (r x) (s h e) -> p r (x s) h e", r=2, h=2, e=EMBED)
        hot_one = moving[0:HOT_K, FIELDS - 2 * HOT_STEPS : FIELDS, :].rearrange("p (r s) b -> p r s b", r=2)

        projected = pb("projected", [P, PROJECT_RING, 2, BATCH])
        turned = pb("turned", [P, BATCH])
        z_sum = pb("z_sum", [P, BATCH])
        free_banks = [projected[:, r, k, :] for r in range(PROJECT_RING) for k in (0, 1)]
        h1_banks = [turned[:]] + free_banks[: HIDDEN1 // P - 1]
        h2_banks = free_banks[HIDDEN1 // P - 1 :][: HIDDEN2 // P]

        ids_loaded = sem("ids_loaded")
        hot_ids_loaded = [sem(f"hot_ids_loaded_{h}") for h in range(HOT_FIELDS)]
        hot_loaded = [sem(f"hot_loaded_{h}") for h in range(HOT_FIELDS)]
        mlp_loaded = sem("mlp_loaded")
        rows_gathered = [sem(f"rows_gathered_{k}") for k in range(GATHER_RING)]
        w_loaded = [sem(f"w_loaded_{k}") for k in range(RAW_RING)]
        pool_made = sem("pool_made")
        identity_made = sem("identity_made")
        fold_made = sem("fold_made")
        selector_zeroed = sem("selector_zeroed")
        selector_made = sem("selector_made")
        hot_hi_made = sem("hot_hi_made")
        hot_lo_made = sem("hot_lo_made")
        hot_one_made = sem("hot_one_made")
        hot_numbers_made = sem("hot_numbers_made")
        hot_used = sem("hot_used")
        w_hi_made = sem("w_hi_made")
        w_lo_by_vector = sem("w_lo_by_vector")
        w_lo_by_gpsimd = sem("w_lo_by_gpsimd")
        e_hi_made = sem("e_hi_made")
        e_lo_made = sem("e_lo_made")
        turn_done = sem("turn_done")
        turn_copied = sem("turn_copied")
        factor_added = sem("factor_added")
        odd_made = sem("odd_made")
        project_done = sem("project_done")
        multiply_done = sem("multiply_done")
        reduce_done = sem("reduce_done")
        z_copied = sem("z_copied")
        h1_summed = sem("h1_summed")
        z_cleared = sem("z_cleared")
        mlp_hi_made = sem("mlp_hi_made")
        mlp_lo_made = sem("mlp_lo_made")
        last_z_made = sem("last_z_made")
        last_z_hi_made = sem("last_z_hi_made")
        last_z_lo_made = sem("last_z_lo_made")
        h1_made = sem("h1_made")
        h1_hi_made = sem("h1_hi_made")
        h1_lo_made = sem("h1_lo_made")
        h2_summed = sem("h2_summed")
        h2_by_scalar = sem("h2_by_scalar")
        h2_by_vector = sem("h2_by_vector")
        y_summed = sem("y_summed")
        y_made = sem("y_made")
        y_stored = sem("y_stored")
        MLP_LOADS = 5 + COL_TILES

        def rows_ready(m):
            turns, slot = divmod(GATHERED.index(m), GATHER_RING)
            return rows_gathered[slot], 16 * 2 * BLOCKS * (turns + 1)

        def rows_of(m):
            return rows[:, GATHERED.index(m) % GATHER_RING, :, :]

        def parts_of(m):
            return parts[:, GATHERED.index(m) % 2, :, :, :, :]

        def before(m, n):
            k = GATHERED.index(m) - n
            return GATHERED[k] if k >= 0 else None

        def nth_gathered(m):
            return GATHERED.index(m) + 1

        def factor_ready(m):
            if m < ADD_FROM:
                return turn_copied, turn_number(m, "partner")
            return factor_added, 2 * (m - ADD_FROM + 1)

        def bank_of(number):
            return z_sum[:] if in_z_bank(number) else turned[:]

        def lo_ready(c):
            by_gpsimd = c in GPSIMD_CHUNKS
            count = sum((n in GPSIMD_CHUNKS) == by_gpsimd for n in range(c + 1))
            return (w_lo_by_gpsimd if by_gpsimd else w_lo_by_vector), count

        def raw_ready(c):
            return w_loaded[c % RAW_RING], 32 * (c // RAW_RING + 1)

        block = ctx.enter_context(nc.Block())

        @block.sync
        def _(sp):
            sp.dma_start(ids_sb[:], ids).then_inc(ids_loaded, 16)

            def load_hot(h):
                sp.dma_start(
                    hot_raw[h], tables[HOT_CHOICE[h]].rearrange("(p s) e -> p (s e)", s=HOT_STEPS)
                ).then_inc(hot_loaded[h], 16)

            def load_weights(c):
                if c >= RAW_RING:
                    sp.wait_ge(w_hi_made, c - RAW_RING + 1)
                    sp.wait_ge(*lo_ready(c - RAW_RING))
                for half in (0, 1):
                    sp.dma_start(
                        w_raw[half * EMBED : (half + 1) * EMBED, c % RAW_RING, :],
                        weights[:, c * CHUNK_COLS : (c + 1) * CHUNK_COLS],
                    ).then_inc(w_loaded[c % RAW_RING], 16)

            def load_mlp():
                sp.wait_ge(hot_one_made, HOT_STEPS * len(HOT_COUPLES))
                sp.wait_ge(hot_hi_made, HOT_FIELDS)
                sp.dma_start(w1_sb[:], w1).then_inc(mlp_loaded, 16)
                sp.dma_start(w2_sb[:], w2).then_inc(mlp_loaded, 16)
                sp.dma_start(w3_sb[:], w3).then_inc(mlp_loaded, 16)
                sp.dma_start(b1_sb[:], b1).then_inc(mlp_loaded, 16)
                sp.dma_start(b2_sb[:], b2).then_inc(mlp_loaded, 16)
                sp.wait_ge(z_cleared, 1)
                for quadrant in range(COL_TILES):
                    row = 32 * quadrant + 2 * LAST_STEPS
                    sp.dma_start(
                        z[row : row + FREE_ROWS, Z_TILES - 1, :],
                        dense[quadrant * FREE_ROWS : (quadrant + 1) * FREE_ROWS, :],
                    ).then_inc(mlp_loaded, 16)

            for h in range(HOT_FIELDS):
                load_hot(h)
            for c in range(N_CHUNKS):
                load_weights(c)
                if c == 11:
                    load_mlp()
            sp.wait_ge(y_made, 1)
            sp.dma_start(out, y[:]).then_inc(y_stored, 16)
            sp.wait_ge(y_stored, 16)

        @block.gpsimd
        def _(pool):
            nc.gpsimd.iota(row_number[:], pattern=[[1, HOT_STEPS]], base=0, channel_multiplier=HOT_STEPS,
                           allow_small_or_imprecise_dtypes=True).then_inc(pool_made, 1)
            pool.memset(identity[:], 0.0).then_inc(pool_made, 1)
            pool.wait_ge(pool_made, 2)
            nc.gpsimd.affine_select(
                out=identity[:], in_=identity[:], compare_op=ALU.not_equal, fill=1.0,
                base=0, pattern=[[-1, P]], channel_multiplier=1,
            ).then_inc(identity_made, 1)
            pool.memset(selector[:], 0.0).then_inc(selector_zeroed, 1)
            pool.wait_ge(selector_zeroed, 1)
            flat = selector[:].rearrange("p k r -> p (k r)")
            pool.memset(flat[0:EMBED, 0 :: 34][:, 0:Z_TILE_STEPS], 1.0).then_inc(selector_made, 1)
            pool.memset(flat[EMBED:P, 1 :: 34][:, 0:Z_TILE_STEPS], 1.0).then_inc(selector_made, 1)
            pool.wait_ge(selector_made, 2)
            pool.wait_ge(ids_loaded, 16)

            def split_weights_lo(c):
                pool.wait_ge(w_hi_made, c + 1)
                if c >= SPLIT_RING:
                    pool.wait_ge(project_done, (c - SPLIT_RING + 1) * GROUPS_PER_CHUNK)
                nc.gpsimd.tensor_tensor(
                    w_lo[:, c % SPLIT_RING, :], w_raw[:, c % RAW_RING, :],
                    w_hi[:, c % SPLIT_RING, :].bitcast(fp32), ALU.subtract,
                ).then_inc(w_lo_by_gpsimd, 1)

            for m in GATHERED:
                if (old := before(m, GATHER_RING)) is not None:
                    pool.wait_ge(e_hi_made, nth_gathered(old))
                    pool.wait_ge(e_lo_made, nth_gathered(old))
                    if old < ADD_FROM:
                        pool.wait_ge(turn_done, done_number(old, "partner"))
                if m == GATHERED[4]:
                    pool.wait_ge(hot_lo_made, HOT_FIELDS)
                    pool.memset(z[:, Z_TILES - 1, :], 0.0).then_inc(z_cleared, 1)
                    pool.wait_ge(z_cleared, 1)
                for f in (0, 1):
                    field = FIELD_AT[2 * m + f]
                    for b in range(BLOCKS):
                        nc.gpsimd.indirect_dma_start(
                            rows_of(m)[:, b, f * EMBED : (f + 1) * EMBED], None,
                            tables[field],
                            bass.IndirectOffsetOnAxis(ap=ids_sb[:, b, field : field + 1], axis=0),
                        ).then_inc(rows_ready(m)[0], 16)
                    for c, fields_before in GPSIMD_CHUNKS.items():
                        if fields_before == 2 * GATHERED.index(m) + f + 1:
                            split_weights_lo(c)

            for done, (low, whole, high) in enumerate(
                [(w1_lo, w1_sb[:], w1_hi), (w2_lo, w2_sb[:], w2_hi)]
                + [(z_lo[:, t, :], z[:, t, :], z_hi[:, t, :]) for t in range(Z_TILES - 1)]
            ):
                pool.wait_ge(mlp_hi_made, done + 1)
                nc.gpsimd.tensor_tensor(low, whole, high.bitcast(fp32), ALU.subtract).then_inc(mlp_lo_made, 1)

        @block.scalar
        def _(act):
            def split_hot_hi(h):
                act.wait_ge(hot_loaded[h], 16)
                if h >= 2:
                    act.wait_ge(hot_used, HOT_STEPS * (h // 2))
                nc.scalar.activation(
                    hot_parts[:, h % 2, :, 0, :],
                    hot_raw[h].rearrange("p (s e) -> p s e", e=EMBED), ACT.Copy,
                ).then_inc(hot_hi_made, 1)

            def split_weights_hi(c):
                act.wait_ge(*raw_ready(c))
                if c >= SPLIT_RING:
                    act.wait_ge(project_done, (c - SPLIT_RING + 1) * GROUPS_PER_CHUNK)
                nc.scalar.activation(
                    w_hi[:, c % SPLIT_RING, :], w_raw[:, c % RAW_RING, :], ACT.Copy
                ).then_inc(w_hi_made, 1)

            def split_rows_hi(m):
                act.wait_ge(*rows_ready(m))
                if (old := before(m, 2)) is not None:
                    act.wait_ge(turn_done, done_number(old, 1))
                nc.scalar.activation(
                    parts_of(m)[:, :, :, 0, :],
                    rows_of(m).rearrange("p b (f e) -> p b f e", f=2),
                    ACT.Copy,
                ).then_inc(e_hi_made, 1)

            def copy_partner(m):
                act.wait_ge(turn_done, done_number(m, "partner"))
                if last_group(False, m - PARTNER_RING) >= 0:
                    act.wait_ge(multiply_done, last_group(False, m - PARTNER_RING) + 1)
                source = bank_of(turn_number(m, "partner"))
                nc.scalar.activation(factors[:, m % PARTNER_RING, :], source, ACT.Copy).then_inc(turn_copied, 1)

            def copy_moving(m, f):
                if is_look_up(m, f):
                    act.wait_ge(hot_used, HOT_STEPS * (HOT_COUPLES.index(m) + 1))
                else:
                    act.wait_ge(turn_done, done_number(m, f))
                source = bank_of(turn_number(m, f))
                nc.scalar.activation(moving[:, 2 * m + f, :], source, ACT.Copy).then_inc(turn_copied, 1)

            def copy_odd(quad):
                for m in (2 * quad, 2 * quad + 1):
                    act.wait_ge(*factor_ready(m))
                if quad >= 1:
                    act.wait_ge(multiply_done, last_group(True, quad - 1) + 1)
                ab, cd = (2 * quad) % PARTNER_RING, (2 * quad + 1) % PARTNER_RING
                low, high = slice(0, EMBED), slice(EMBED, P)
                for slot, half, source in (
                    (ODD_SLOTS[0], low, factors[high, ab, :]), (ODD_SLOTS[0], high, factors[low, cd, :]),
                    (ODD_SLOTS[1], low, factors[low, ab, :]), (ODD_SLOTS[1], high, factors[low, cd, :]),
                ):
                    nc.scalar.activation(factors[half, slot, :], source, ACT.Copy).then_inc(odd_made, 1)

            def copy_z(t):
                act.wait_ge(reduce_done, min(BATCHES, Z_TILE_STEPS * (t + 1)))
                nc.scalar.activation(z[:, t, :], z_sum[:], ACT.Copy).then_inc(z_copied, 1)

            def split_mlp_hi(high, whole, place):
                act.wait_ge(project_done, last_projected(place) + 1)
                nc.scalar.activation(high, whole, ACT.Copy).then_inc(mlp_hi_made, 1)

            for h in range(HOT_FIELDS):
                act.dma_start(hot_id[:, h, :], hot_ids[h : h + 1, :].to_broadcast([HOT_K, BATCH])).then_inc(
                    hot_ids_loaded[h], 16
                )
            split_hot_hi(0)
            split_hot_hi(1)
            act.wait_ge(identity_made, 1)
            nc.scalar.activation(identity_r[:], identity[:], ACT.Copy).then_inc(fold_made, 1)
            for half, cols in ((slice(0, EMBED), 0), (slice(EMBED, P), EMBED)):
                nc.scalar.activation(
                    fold[half, EMBED : 2 * EMBED], identity[half, cols : cols + EMBED], ACT.Copy
                ).then_inc(fold_made, 1)
                for side in (0, 2):
                    nc.scalar.activation(
                        fold[half, side * EMBED : (side + 1) * EMBED],
                        identity[half, EMBED - cols : 2 * EMBED - cols], ACT.Copy,
                    ).then_inc(fold_made, 1)
            split_weights_hi(0)
            copy_moving(0, 0)
            copy_moving(0, 1)
            split_hot_hi(2)
            split_hot_hi(3)
            split_rows_hi(1)
            copy_partner(0)
            copy_partner(1)
            copy_odd(0)
            copy_moving(1, 0)
            copy_moving(1, 1)
            split_weights_hi(1)
            for g in range(N_GROUPS):
                for c in CHUNK_AT[g]:
                    split_weights_hi(c)
                for q in HOT_AT[g]:
                    for f in (0, 1):
                        copy_moving(HOT_COUPLES[q], f)
                for m in SPLIT_AT[g]:
                    split_rows_hi(m)
                for m in PARTNER_AT[g]:
                    copy_partner(m)
                for quad in ODD_AT[g]:
                    copy_odd(quad)
                for m, f in MOVING_AT[g]:
                    copy_moving(m, f)
                for t in range(Z_TILES - 1):
                    if g == 2 * (Z_TILE_STEPS * (t + 1) - 1) + 3:
                        copy_z(t)
            act.wait_ge(mlp_loaded, 16 * MLP_LOADS)
            split_mlp_hi(w1_hi, w1_sb[:], 3)
            split_mlp_hi(w2_hi, w2_sb[:], 5)
            for t in range(Z_TILES - 1):
                split_mlp_hi(z_hi[:, t, :], z[:, t, :], 6 + t)
            act.wait_ge(last_z_made, 1)
            nc.scalar.activation(z_hi[:, Z_TILES - 1, :], z[:, Z_TILES - 1, :], ACT.Copy).then_inc(last_z_hi_made, 1)

            for n in range(HIDDEN1 // P):
                act.wait_ge(h1_made, n + 1)
                nc.scalar.activation(h1_hi[:, n, :], h1[:, n, :], ACT.Copy).then_inc(h1_hi_made, 1)
            act.wait_ge(h2_summed, 1)
            nc.scalar.activation(
                h2[:, 0, :], h2_banks[0], ACT.Relu, bias=b2_sb[:, 0:1]
            ).then_inc(h2_by_scalar, 1)

        @block.vector
        def _(dve):
            def split_hot_lo(h):
                dve.wait_ge(hot_hi_made, h + 1)
                nc.vector.tensor_tensor(
                    hot_parts[:, h % 2, :, 1, :],
                    hot_raw[h].rearrange("p (s e) -> p s e", e=EMBED),
                    hot_parts[:, h % 2, :, 0, :].bitcast(fp32), ALU.subtract,
                ).then_inc(hot_lo_made, 1)

            def make_hot_numbers(q):
                for h in (2 * q, 2 * q + 1):
                    dve.wait_ge(hot_ids_loaded[h], 16)
                couple = slice(2 * q, 2 * q + 2)
                nc.vector.tensor_copy(hot_number[:, couple, :], hot_id[:, couple, :]).then_inc(hot_numbers_made, 1)

            def make_hot_ones(q, steps):
                dve.wait_ge(hot_numbers_made, q + 1)
                for s in steps:
                    if q >= 1:
                        dve.wait_ge(hot_used, HOT_STEPS * (q - 1) + s + 1)
                    nc.vector.tensor_scalar(
                        hot_one[:, :, s, :], hot_number[:, 2 * q : 2 * q + 2, :],
                        row_number[0:HOT_K, s : s + 1], None, ALU.is_equal,
                    ).then_inc(hot_one_made, 1)

            def split_weights_lo(c):
                dve.wait_ge(w_hi_made, c + 1)
                if c >= SPLIT_RING:
                    dve.wait_ge(project_done, (c - SPLIT_RING + 1) * GROUPS_PER_CHUNK)
                nc.vector.tensor_tensor(
                    w_lo[:, c % SPLIT_RING, :], w_raw[:, c % RAW_RING, :],
                    w_hi[:, c % SPLIT_RING, :].bitcast(fp32), ALU.subtract,
                ).then_inc(w_lo_by_vector, 1)

            def split_rows_lo(m):
                dve.wait_ge(e_hi_made, nth_gathered(m))
                nc.vector.tensor_tensor(
                    parts_of(m)[:, :, :, 1, :],
                    rows_of(m).rearrange("p b (f e) -> p b f e", f=2),
                    parts_of(m)[:, :, :, 0, :].bitcast(fp32), ALU.subtract,
                ).then_inc(e_lo_made, 1)

            def add_factor(m, f):
                dve.wait_ge(turn_copied, turn_number(m, f))
                dve.wait_ge(multiply_done, last_group(False, m - PARTNER_RING) + 1)
                nc.vector.tensor_tensor(
                    factors[f * EMBED : (f + 1) * EMBED, m % PARTNER_RING, :],
                    turned[0:EMBED, :], moving[EMBED:P, 2 * m + f, :].bitcast(fp32), ALU.add,
                ).then_inc(factor_added, 1)

            def multiply(g):
                for tile in GROUPS[g]:
                    if is_odd(tile):
                        dve.wait_ge(odd_made, 4 * (tile[3] + 1))
                    else:
                        dve.wait_ge(*factor_ready(tile[3]))
                first, second = (tile[2] for tile in GROUPS[g])
                if first == second:
                    factor = factors[:, first : first + 1, :].to_broadcast([P, 2, BATCH])
                else:
                    factor = factors[:, first : second + 1 : second - first, :]
                if g >= PRODUCT_RING:
                    dve.wait_ge(reduce_done, (g - PRODUCT_RING) // 2 + 1)
                dve.wait_ge(project_done, g + 1)
                nc.vector.tensor_tensor(
                    product[:, g % PRODUCT_RING, :, :], projected[:, g % PROJECT_RING, :, :], factor, ALU.mult
                ).then_inc(multiply_done, 1)

            dve.wait_ge(pool_made, 1)
            make_hot_numbers(0)
            make_hot_ones(0, range(2))
            split_hot_lo(0)
            split_hot_lo(1)
            make_hot_ones(0, range(2, HOT_STEPS))
            split_weights_lo(0)
            make_hot_numbers(1)
            make_hot_ones(1, range(2))
            split_rows_lo(1)
            split_hot_lo(2)
            split_hot_lo(3)
            make_hot_ones(1, range(2, HOT_STEPS))
            split_weights_lo(1)
            for g in range(N_GROUPS):
                for c in CHUNK_AT[g]:
                    if c not in GPSIMD_CHUNKS:
                        split_weights_lo(c)
                for m in SPLIT_AT[g]:
                    split_rows_lo(m)
                multiply(g)
                for m, f in MOVING_AT[g]:
                    if m >= ADD_FROM:
                        add_factor(m, f)

            dve.wait_ge(mlp_loaded, 16 * MLP_LOADS)
            dve.wait_ge(reduce_done, BATCHES)
            last_z = z[:, Z_TILES - 1, :]
            nc.vector.tensor_tensor(last_z, z_sum[:], last_z, ALU.add).then_inc(last_z_made, 1)
            dve.wait_ge(last_z_hi_made, 1)
            nc.vector.tensor_tensor(
                z_lo[:, Z_TILES - 1, :], last_z, z_hi[:, Z_TILES - 1, :].bitcast(fp32), ALU.subtract
            ).then_inc(last_z_lo_made, 1)

            def relu_h1(n):
                dve.wait_ge(h1_summed, n + 1)
                nc.vector.tensor_scalar(
                    h1[:, n, :], h1_banks[n], b1_sb[:, n : n + 1], 0.0, ALU.add, ALU.max
                ).then_inc(h1_made, 1)

            def split_h1_lo(n):
                dve.wait_ge(h1_hi_made, n + 1)
                nc.vector.tensor_tensor(
                    h1_lo[:, n, :], h1[:, n, :], h1_hi[:, n, :].bitcast(fp32), ALU.subtract
                ).then_inc(h1_lo_made, 1)

            relu_h1(0)
            for n in range(1, HIDDEN1 // P):
                if n == 1:
                    relu_h1(n)
                split_h1_lo(n - 1)
                if n > 1:
                    relu_h1(n)
            split_h1_lo(HIDDEN1 // P - 1)
            dve.wait_ge(h2_summed, 2)
            nc.vector.tensor_scalar(
                h2[:, 1, :], h2_banks[1], b2_sb[:, 1:2], 0.0, ALU.add, ALU.max
            ).then_inc(h2_by_vector, 1)
            dve.wait_ge(y_summed, 1)
            nc.vector.tensor_copy(y[:], z_sum[0:1, :]).then_inc(y_made, 1)

        @block.tensor
        def _(pe):
            def take_bank(number):
                old = bank_free_at(number)
                if old >= 1:
                    pe.wait_ge(turn_copied, old)
                    m, f = TURNS[old - 1]
                    if m >= ADD_FROM:
                        pe.wait_ge(factor_added, 2 * (m - ADD_FROM) + f + 1)

            def turn_partner(m):
                pe.wait_ge(*rows_ready(m))
                number = turn_number(m, "partner")
                take_bank(number)
                for b in range(BLOCKS):
                    last = nc.tensor.transpose(
                        bank_of(number)[:, b * P : (b + 1) * P], rows_of(m)[:, b, :], identity[:]
                    )
                last.then_inc(turn_done, 1)

            def turn_moving(m, f):
                pe.wait_ge(e_lo_made, nth_gathered(m))
                number = turn_number(m, f)
                take_bank(number)
                for b in range(BLOCKS):
                    last = nc.tensor.matmul(
                        bank_of(number)[:, b * P : (b + 1) * P],
                        parts_of(m)[:, b, f, :, :].rearrange("p h e -> p (h e)"), identity_r[:],
                        start=True, stop=True,
                    )
                last.then_inc(turn_done, 1)

            def look_up_hot(q):
                pe.wait_ge(hot_lo_made, 2 * q + 2)
                m = HOT_COUPLES[q]
                for f in (0, 1):
                    take_bank(turn_number(m, f))
                for s in range(HOT_STEPS):
                    pe.wait_ge(hot_one_made, HOT_STEPS * q + s + 1)
                    for f in (0, 1):
                        last = nc.tensor.matmul(
                            bank_of(turn_number(m, f)),
                            hot_parts[:, f, s, :, :].rearrange("p h e -> p (h e)"), hot_one[:, f, s, :],
                            start=(s == 0), stop=(s == HOT_STEPS - 1),
                        )
                    last.then_inc(hot_used, 1)

            def fold_partner(m):
                pe.wait_ge(fold_made, 7)
                pe.wait_ge(turn_copied, moving_number(2 * m + 1))
                take_bank(turn_number(m, "partner"))
                for f in (0, 1):
                    last = nc.tensor.matmul(
                        bank_of(turn_number(m, "partner")),
                        fold[:, (1 - f) * EMBED : (1 - f) * EMBED + P], moving[:, 2 * m + f, :],
                        start=(f == 0), stop=(f == 1),
                    )
                last.then_inc(turn_done, 1)

            def project(g):
                pe.wait_ge(turn_copied, max(moving_number(tile[0]) for tile in GROUPS[g]))
                pe.wait_ge(*lo_ready(g // GROUPS_PER_CHUNK))
                if g >= PROJECT_RING:
                    pe.wait_ge(multiply_done, g - PROJECT_RING + 1)
                for k, tile in enumerate(GROUPS[g]):
                    c, col = divmod((2 * g + k) * P, CHUNK_COLS)
                    for w in (w_hi, w_lo):
                        last = nc.tensor.matmul(
                            projected[:, g % PROJECT_RING, k, :],
                            w[:, c % SPLIT_RING, col : col + P],
                            moving[:, tile[0], :],
                            start=(w is w_hi), stop=(w is w_lo),
                        )
                last.then_inc(project_done, 1)

            def reduce(batch):
                t, step = divmod(batch, Z_TILE_STEPS)
                pe.wait_ge(multiply_done, 2 * batch + 2)
                if batch == 0:
                    pe.wait_ge(turn_copied, LAST_IN_Z_BANK)
                if step == 0 and t >= 1:
                    pe.wait_ge(z_copied, t)
                end = step == Z_TILE_STEPS - 1 or batch == BATCHES - 1
                for quadrant in range(COL_TILES):
                    tile = COL_TILES * batch + quadrant
                    last = nc.tensor.matmul(
                        z_sum[32 * quadrant : 32 * quadrant + 32, :],
                        selector[:, step, :],
                        product[:, tile // 2 % PRODUCT_RING, tile % 2, :],
                        start=(step == 0), stop=end, tile_position=(0, 32 * quadrant),
                    )
                last.then_inc(reduce_done, 1)

            def multiply_parts(bank, weights, values, start, stop):
                for k, (a, b) in enumerate(((0, 0), (0, 1), (1, 0))):
                    last = nc.tensor.matmul(
                        bank, weights[a], values[b], start=(start and k == 0), stop=(stop and k == 2)
                    )
                return last

            def add_to_h1(n, z_tiles):
                for t in z_tiles:
                    last = multiply_parts(
                        h1_banks[n], [w[:, t, n * P : (n + 1) * P] for w in (w1_hi, w1_lo)],
                        [z_hi[:, t, :], z_lo[:, t, :]], t == 0, t == Z_TILES - 1,
                    )
                if t == Z_TILES - 1:
                    last.then_inc(h1_summed, 1)

            def add_to_h2(n, t):
                last = multiply_parts(
                    h2_banks[n], [w[:, t, n * P : (n + 1) * P] for w in (w2_hi, w2_lo)],
                    [h1_hi[:, t, :], h1_lo[:, t, :]], t == 0, t == HIDDEN1 // P - 1,
                )
                if t == HIDDEN1 // P - 1:
                    last.then_inc(h2_summed, 1)

            pe.wait_ge(identity_made, 1)
            for _ in range(WARM_UPS):
                nc.tensor.matmul(projected[:, 0, 0, 0:P], identity[:], identity[:], start=True, stop=True)
            look_up_hot(0)
            fold_partner(0)
            turn_partner(1)
            turn_moving(1, 0)
            turn_moving(1, 1)
            pe.wait_ge(selector_made, 2)
            for g in range(N_GROUPS):
                for q in HOT_AT[g]:
                    look_up_hot(q)
                for m in PARTNER_AT[g]:
                    if m in GATHERED:
                        turn_partner(m)
                    else:
                        fold_partner(m)
                project(g)
                for m, f in MOVING_AT[g]:
                    turn_moving(m, f)
                if g % 2 == 1 and g >= 3:
                    reduce((g - 3) // 2)
            pe.wait_ge(mlp_lo_made, 2 + Z_TILES - 1)
            take_bank(len(TURNS) + 1)
            add_to_h1(0, range(Z_TILES - 1))
            reduce(BATCHES - 1)
            add_to_h1(1, range(Z_TILES - 1))
            pe.wait_ge(last_z_lo_made, 1)
            add_to_h1(0, [Z_TILES - 1])
            add_to_h1(1, [Z_TILES - 1])
            for n in range(2, HIDDEN1 // P):
                add_to_h1(n, range(Z_TILES))
            pe.wait_ge(mlp_loaded, 16 * MLP_LOADS)
            for t in range(HIDDEN1 // P):
                pe.wait_ge(h1_lo_made, t + 1)
                for n in range(HIDDEN2 // P):
                    add_to_h2(n, t)
            for t, half_made in enumerate((h2_by_scalar, h2_by_vector)):
                pe.wait_ge(half_made, 1)
                last = nc.tensor.matmul(
                    z_sum[0:1, :], w3_sb[:, t : t + 1], h2[:, t, :],
                    start=(t == 0), stop=(t == HIDDEN2 // P - 1),
                )
            last.then_inc(y_summed, 1)


def kernel(**inputs):
    import concourse.bacc as bacc
    from concourse.bass_utils import run_bass_kernel_spmd

    given = {name: np.asarray(a) for name, a in inputs.items()}
    arrays = {}
    arrays["ids"] = np.ascontiguousarray(given["ids"].reshape(BLOCKS, P, FIELDS).transpose(1, 0, 2))
    arrays["hot_ids"] = np.ascontiguousarray(given["ids"].T[HOT_CHOICE])
    for f in range(FIELDS):
        arrays[f"tbl_{f}"] = np.ascontiguousarray(given[f"tbl_{f}"])

    w = given["L0_rec_w"]
    both_ways = np.concatenate([w.transpose(1, 0, 2), w.transpose(2, 0, 1)], axis=1)
    picked = []
    row_of = np.zeros((Z_TILES, P), np.int64)
    for n, (place, partners, _, _) in enumerate(TILES):
        for half, partner in enumerate(partners):
            moved, other = FIELD_AT[place], FIELD_AT[partner]
            pair = pair_index(min(moved, other), max(moved, other))
            picked.append(pair if moved < other else PAIRS + pair)
            row_of[z_place(n, half)] = pair
    for d in range(DENSE):
        row_of[Z_TILES - 1, 32 * (d // FREE_ROWS) + 2 * LAST_STEPS + d % FREE_ROWS] = PAIRS + d
    arrays["weights"] = np.ascontiguousarray(both_ways[:, picked, :]).reshape(EMBED, -1)
    arrays["w1"] = np.ascontiguousarray(given["W_top1"][row_of.T])
    arrays["w2"] = np.ascontiguousarray(given["W_top2"].reshape(-1, P, HIDDEN2).transpose(1, 0, 2))
    arrays["w3"] = np.ascontiguousarray(given["W_top3"].reshape(-1, P).T)
    arrays["b1"] = np.ascontiguousarray(given["b_top1"].reshape(-1, P).T)
    arrays["b2"] = np.ascontiguousarray(given["b_top2"].reshape(-1, P).T)
    arrays["dense"] = np.ascontiguousarray(given["dense_ctx"].T)

    nc = bacc.Bacc("TRN2", target_bir_lowering=False, num_devices=1)
    aps = {
        name: nc.dram_tensor(f"in_{name}", a.shape, mybir.dt.from_np(a.dtype), kind="ExternalInput").ap()
        for name, a in arrays.items()
    }
    out = nc.dram_tensor("out_y", (1, BATCH), mybir.dt.float32, kind="ExternalOutput").ap()
    build_tower(
        nc, aps["ids"], aps["hot_ids"], [aps[f"tbl_{f}"] for f in range(FIELDS)], aps["weights"],
        aps["w1"], aps["b1"], aps["w2"], aps["b2"], aps["w3"], aps["dense"], out,
    )
    result = run_bass_kernel_spmd(nc, [{f"in_{name}": a for name, a in arrays.items()}], core_ids=[0])
    return result.results[0]["out_y"].reshape(BATCH, 1)
```
